# Optimizing a Trainium2 kernel written in Bass

```python
import numpy as np
import jax
import jax.numpy as jnp

def _softmax(x, axis=-1):
    return jax.nn.softmax(x, axis=axis)

def _gelu(x):
    return jax.nn.gelu(x, approximate=True)

def _silu(x):
    return jax.nn.silu(x)

def _sigmoid(x):
    return jax.nn.sigmoid(x)

def _layernorm(x, axis=-1, eps=1e-05):
    m = jnp.mean(x, axis=axis, keepdims=True)
    v = jnp.var(x, axis=axis, keepdims=True)
    return (x - m) / jnp.sqrt(v + eps)

def _scatter_add(tgt, idx, src, axis=0):
    return tgt.at[idx].add(src)

def _segment_sum(src, seg, n):
    return jax.ops.segment_sum(src, seg, n)
kernel_name = 'mk_adaln_ffn_d1_seqx_r4_da1406'

def setup_inputs(seed: int=0):
    np.random.seed(seed)
    _w = jnp.asarray

    def _rec_inputs():
        import jax
        import jax.numpy as jnp
        _rk = jax.random.key(seed)
        x = -0.0003929 + 0.9999 * jax.random.normal(jax.random.fold_in(_rk, 1), (128, 64, 1024), jnp.float32)
        _lenS = 64 - jax.random.randint(jax.random.fold_in(_rk, 7), (128,), 0, max(1, 64 // 4) + 1, jnp.int32)
        _lenS2 = 64 - jax.random.randint(jax.random.fold_in(_rk, 8), (128,), 0, max(1, 64 // 4) + 1, jnp.int32)
        itok_B_8_3872 = jax.random.randint(jax.random.fold_in(_rk, 11), (128,), 8, 3873, jnp.int32)
        return (x, itok_B_8_3872)
    x, itok_B_8_3872 = _rec_inputs()

    def _L0_cond_setup():
        import math
        import jax, jax.numpy as jnp
        import numpy as np
        H, N, B, L = (64, 64, 16, 1024)
        DT_MIN, DT_MAX = (0.001, 0.1)

        def _get_kernel(log_dt, C, log_A_real, A_imag, length):
            Cc = C[..., 0] + 1j * C[..., 1]
            dt = jnp.exp(log_dt)
            A = -jnp.exp(log_A_real) + 1j * A_imag
            dtA = A * dt[:, None]
            P = dtA[:, :, None] * jnp.arange(length, dtype=jnp.float32)
            Cs = Cc * (jnp.exp(dtA) - 1.0) / A
            K = 2.0 * jnp.einsum('hn,hnl->hl', Cs, jnp.exp(P)).real
            return K
        key = jax.random.key(seed)
        ks = jax.random.split(key, 6)
        u = jax.random.normal(ks[0], (B, H, L), dtype=jnp.float32)
        length = jax.random.randint(ks[1], (B,), 0, L)
        log_dt = jax.random.uniform(ks[2], (H,), dtype=jnp.float32) * (math.log(DT_MAX) - math.log(DT_MIN)) + math.log(DT_MIN)
        C = jax.random.normal(ks[3], (H, N, 2), dtype=jnp.float32)
        log_A_real = jnp.log(0.5 * jnp.ones((H, N), dtype=jnp.float32))
        A_imag = math.pi * jnp.broadcast_to(jnp.arange(N, dtype=jnp.float32), (H, N))
        D = jax.random.normal(ks[4], (H,), dtype=jnp.float32)
        return {'u': u, 'length': length, 'log_dt': log_dt, 'C': C, 'log_A_real': log_A_real, 'A_imag': A_imag, 'D': D}
    _L0_cond_all = _L0_cond_setup()
    _L0_cond_in = {k: v for k, v in _L0_cond_all.items() if k in ('log_dt', 'C', 'log_A_real', 'A_imag', 'D')}
    del _L0_cond_all

    def _L0_ffn_setup():
        import jax, jax.numpy as jnp
        import numpy as np
        R = 16
        LORA_ALPHA = 16
        SCALING = LORA_ALPHA / R
        key = jax.random.key(seed)
        kx, kr, ka = jax.random.split(key, 3)
        B, S, D, DO, E = (4, 512, 1024, 1024, 8)
        x = jax.random.normal(kx, (B, S, D), dtype=jnp.float32)
        bound_r = 1.0 / np.sqrt(D)
        route_w = jax.random.uniform(kr, (E, D), jnp.float32, -bound_r, bound_r)
        bound_a = 1.0 / np.sqrt(D)
        A = jax.random.uniform(ka, (E, R, D), jnp.float32, -bound_a, bound_a)
        kb = jax.random.fold_in(key, 7)
        Bw = jax.random.normal(kb, (E, DO, R), dtype=jnp.float32) * 0.02
        return {'x': x, 'route_w': route_w, 'A': A, 'Bw': Bw}
    _L0_ffn_all = _L0_ffn_setup()
    _L0_ffn_in = {k: v for k, v in _L0_ffn_all.items() if k in ('route_w', 'A', 'Bw')}
    del _L0_ffn_all
    return {'x': x, 'itok_B_8_3872': itok_B_8_3872, 'L0_cond_log_dt': _L0_cond_in['log_dt'], 'L0_cond_C': _L0_cond_in['C'], 'L0_cond_log_A_real': _L0_cond_in['log_A_real'], 'L0_cond_A_imag': _L0_cond_in['A_imag'], 'L0_cond_D': _L0_cond_in['D'], 'L0_ffn_route_w': _L0_ffn_in['route_w'], 'L0_ffn_A': _L0_ffn_in['A'], 'L0_ffn_Bw': _L0_ffn_in['Bw']}

def reference(x, itok_B_8_3872, L0_cond_log_dt, L0_cond_C, L0_cond_log_A_real, L0_cond_A_imag, L0_cond_D, L0_ffn_route_w, L0_ffn_A, L0_ffn_Bw):
    import jax
    import jax.numpy as jnp

    def _L0_cond_ref(u, length, log_dt, C, log_A_real, A_imag, D):
        import math
        import jax, jax.numpy as jnp
        import numpy as np
        H, N, B, L = (64, 64, 16, 1024)
        DT_MIN, DT_MAX = (0.001, 0.1)

        def _get_kernel(log_dt, C, log_A_real, A_imag, length):
            Cc = C[..., 0] + 1j * C[..., 1]
            dt = jnp.exp(log_dt)
            A = -jnp.exp(log_A_real) + 1j * A_imag
            dtA = A * dt[:, None]
            P = dtA[:, :, None] * jnp.arange(length, dtype=jnp.float32)
            Cs = Cc * (jnp.exp(dtA) - 1.0) / A
            K = 2.0 * jnp.einsum('hn,hnl->hl', Cs, jnp.exp(P)).real
            return K
        Bq, Hq, Lq = u.shape
        mask = (jnp.arange(Lq) < length[:, None]).astype(u.dtype)
        u_m = u * mask[:, None, :]
        kernel = _get_kernel(log_dt, C, log_A_real, A_imag, Lq)
        n = 2 * Lq
        k_f = jnp.fft.rfft(kernel, n=n)
        u_f = jnp.fft.rfft(u_m, n=n)
        y = jnp.fft.irfft(u_f * k_f, n=n)[..., :Lq]
        y = y + u_m * D[:, None]
        return y * mask[:, None, :]

    def _L0_ffn_ref(x, route_w, A, Bw):
        import jax, jax.numpy as jnp
        import numpy as np
        R = 16
        LORA_ALPHA = 16
        SCALING = LORA_ALPHA / R
        logits = jnp.einsum('bsd,ed->bse', x, route_w)
        topk_v, topk_idx = jax.lax.top_k(logits, 1)
        E = logits.shape[-1]
        route_weight = jax.nn.one_hot(topk_idx[..., 0], E, dtype=logits.dtype) * topk_v
        h = jnp.einsum('bsd,erd->bser', x, A)
        wh = route_weight[..., None] * h
        out = jnp.einsum('bser,eor->bso', wh, Bw) * SCALING
        return out
    x = x + _L0_ffn_ref(_L0_cond_ref(x, itok_B_8_3872, L0_cond_log_dt, L0_cond_C, L0_cond_log_A_real, L0_cond_A_imag, L0_cond_D), L0_ffn_route_w, L0_ffn_A, L0_ffn_Bw)
    return x

_drawn_inputs = setup_inputs


def setup_inputs(seed=0):
    import zlib

    import numpy as np

    out = dict(_drawn_inputs(seed))
    spreads = {'L0_cond_log_A_real': (-0.6931471824645996, 0.2)}
    factors = {}
    for name, (base, spread) in spreads.items():
        noise = np.random.default_rng([zlib.crc32(name.encode()), seed]).standard_normal(out[name].shape)
        drawn = base * np.exp(spread * noise) if base else spread * noise
        out[name] = jnp.asarray(drawn.astype(out[name].dtype))
    for name, factor in factors.items():
        out[name] = (out[name] * factor).astype(out[name].dtype)
    return out
```

```python
import concourse.bass as bass
import numpy as np
from concourse import mybir
from contextlib import ExitStack


F32 = mybir.dt.float32
F32R = mybir.dt.float32r
I32 = mybir.dt.int32
ALU = mybir.AluOpType
ACT = mybir.ActivationFunctionType
AX = mybir.AxisListType

P = 128
ROUND = 12582912.0
TURN = 6.283185


def conv_ffn_kernel(nc, x, lens, log_dt, Cw, log_A_real, A_imag, D, route_w, Aw, Bw, out):
    B, H, L = x.shape
    N = A_imag.shape[1]
    E, R, _ = Aw.shape
    ER = E * R
    NB = L // P
    NE = NB // 2
    Q = 2 * P
    NS = NE - 1
    NW = ER + E
    HALF = L // 2
    G16 = 16
    assert B == P and 2 * N == P and ER == P and HALF == 512 and H % 4 == 0

    ctx = ExitStack()
    with ctx:
        def sb(name, shape, dt=F32):
            return ctx.enter_context(nc.sbuf_tensor(name, shape, dt))

        def bank(name):
            return ctx.enter_context(nc.psum_tensor(name, [P, 512], F32))

        def sem(name):
            return ctx.enter_context(nc.semaphore(name))

        ident = sb("ident", [P, P])
        swap = sb("swap", [P, P])
        egrid = sb("egrid", [P, Q])
        grid16 = sb("grid16", [P, G16])
        desc = sb("desc", [P, E])
        quarter = sb("quarter", [P, 1])
        sinbias = sb("sinbias", [P, 1])
        clamp_lo = sb("clamp_lo", [P, 1])
        clamp_hi = sb("clamp_hi", [P, 1])
        posn = sb("posn", [P, NB])
        lens_i = sb("lens_i", [P, P], I32)
        lens_f = sb("lens_f", [P, P])
        mask = sb("mask", [P, 2, NE, P])
        zeros = sb("zeros", [1, P])
        Drow = sb("Drow", [1, H])
        route_nat = sb("route_nat", [E, L])
        A_nat = sb("A_nat", [P, L])
        B_nat = sb("B_nat", [P, NB, ER])
        Wt = sb("Wt", [P, NB, NW])
        Bw_hi = sb("Bw_hi", [P, L], F32R)
        Bw_lo = sb("Bw_lo", [P, L], F32R)
        logs = sb("logs", [H, N + 1])
        A_im = sb("A_im", [H, N])
        C_nat = sb("C_nat", [H, N, 2])
        NT = 9
        V, VH, VL, RHO, LR, BM, AM, BR, CK = range(NT)
        pack = sb("pack", [H, NT, 2, N])
        tab = sb("tab", [P, NT, H])
        Ck = sb("Ck", [P, H, 2], F32R)
        rho16 = sb("rho16", [P, H, G16])
        magP = sb("magP", [P, H, G16])
        magQ = sb("magQ", [P, H, G16])
        ex = sb("ex", [H, 5, 2 * N])
        exps = sb("exps", [H, N + 1])
        w = sb("w", [H, N])
        w12 = sb("w12", [H, N], F32R)
        w2 = sb("w2", [H, N])
        v12 = sb("v12", [H, N], F32R)
        tmp = sb("tmp", [H, 11, N])
        phase = sb("phase", [H, 2, N])
        rr = sb("rr", [H, 2 * N])
        er = sb("er", [H, 2 * N])
        sine = sb("sine", [H, 2, N])
        sine_half = sb("sine_half", [H, 2, N])
        cm1 = sb("cm1", [H, 2, N])
        xt = [sb(f"xt{s}", [P, L]) for s in range(4)]
        Xhi = [sb(f"Xhi{s}", [P, 2, HALF], F32R) for s in range(2)]
        Xlo = [sb(f"Xlo{s}", [P, 2, HALF], F32R) for s in range(2)]
        turns_h = [sb(f"turns_h{s}", [P, Q]) for s in range(2)]
        turns_t = [sb(f"turns_t{s}", [P, Q]) for s in range(2)]
        whole = sb("whole", [P, Q])
        frac1 = sb("frac1", [P, Q])
        frac2 = sb("frac2", [P, Q])
        frac = [sb(f"fraction{s}", [P, Q]) for s in range(2)]
        wave = [sb(f"wave_{s}", [P, Q]) for s in range(2)]
        wave1 = sb("wave1", [P, Q])
        Grev = [sb(f"Grev{s}", [P, Q]) for s in range(2)]
        Ghi = [sb(f"Ghi{s}", [P, Q], F32R) for s in range(4)]
        Glo = [sb(f"Glo{s}", [P, Q], F32R) for s in range(4)]
        m1 = [sb(f"m1_{s}", [P, 2, P]) for s in range(2)]
        Mx = [sb(f"Mx{s}", [P, P]) for s in range(2)]
        r1 = [sb(f"r1_{s}", [P, 2, P]) for s in range(2)]
        Rx = [sb(f"Rx{s}", [P, P]) for s in range(2)]
        ck = [sb(f"ck{s}", [P, 2], F32R) for s in range(2)]
        krow = [sb(f"krow{s}", [1, Q]) for s in range(2)]
        Bhi = [sb(f"Bhi{s}", [P, 2, P], F32R) for s in range(2)]
        Blo = [sb(f"Blo{s}", [P, 2, P], F32R) for s in range(2)]
        Traw = [sb(f"Traw{s}", [P, Q]) for s in range(2)]
        Thi = [sb(f"Thi{s}", [P, 2, P], F32R) for s in range(2)]
        Tlo = [sb(f"Tlo{s}", [P, 2, P], F32R) for s in range(2)]
        Sf = [sb(f"Sf{s}", [P, NS * P]) for s in range(2)]
        Shi = [sb(f"Shi{s}", [P, NS * P], F32R) for s in range(2)]
        Slo = [sb(f"Slo{s}", [P, NS * P], F32R) for s in range(2)]
        Y = sb("Y", [P, 2, NE, P])
        top = sb("top", [P, 1])
        rank = sb("rank", [P, E])
        best = sb("best", [P, 1])
        gate = sb("gate", [P, E])
        wh = sb("wh", [P, ER])
        whi = [sb(f"whi{s}", [P, P], F32R) for s in range(2)]
        wlo = [sb(f"wlo{s}", [P, P], F32R) for s in range(2)]
        ost = [sb(f"ost{s}", [P, L]) for s in range(2)]

        kdram = nc.dram_tensor("kdram", [2, P + Q], F32, kind="Internal").ap()

        psX = [bank("psXe"), bank("psXo")]
        psY = [bank("psYe"), bank("psYo")]
        psS = bank("psS")
        psZ = bank("psZ")
        psO = [bank("psO0"), bank("psO1")]
        psK = psO[0][0:1, 0:Q]
        psB = psO[0][:, Q:2 * Q]
        psWh = psZ[:, 256:256 + P]

        in_par = sem("in_par")
        in_len = sem("in_len")
        in_D = sem("in_D")
        in_rw = sem("in_rw")
        in_A = sem("in_A")
        in_B = sem("in_B")
        pad_done = sem("pad_done")
        consts = sem("consts")
        cols_set = sem("cols_set")
        zero_row = sem("zero_row")
        v_set = sem("v_set")
        phases_done = sem("phases_done")
        sines_done = sem("sines_done")
        pack_done = sem("pack_done")
        tabs_turned = sem("tabs_turned")
        tab_done = sem("tab_done")
        ck_hi_done = sem("ck_hi_done")
        ck_done = sem("ck_done")
        rho_done = sem("rho_done")
        mag_done = sem("mag_done")
        mask_done = sem("mask_done")
        w_turned = sem("w_turned")
        w_done = sem("w_done")
        b_turned = sem("b_turned")
        bhi_set = sem("bhi_set")
        blo_set = sem("blo_set")
        x_in = [sem(f"x_in{s}") for s in range(4)]
        k_out = [sem(f"k_out{s}") for s in range(2)]
        t_in = [sem(f"t_in{s}") for s in range(2)]
        o_out = [sem(f"o_out{s}") for s in range(2)]
        turns_done = sem("turns_done")
        whole_done = sem("whole_done")
        frac1_done = sem("frac1_done")
        frac2_done = sem("frac2_done")
        frac_done = sem("frac_done")
        wave_done = sem("wave_done")
        wave1_done = sem("wave1_done")
        grev_done = sem("grev_done")
        ghi_done = sem("ghi_done")
        glo_done = sem("glo_done")
        m1_done = sem("m1_done")
        mx_done = sem("mx_done")
        r1_done = sem("r1_done")
        rx_done = sem("rx_done")
        ckr_done = sem("ckr_done")
        kmm_done = sem("kmm_done")
        krow_done = sem("krow_done")
        bhi_done = sem("bhi_done")
        blo_done = sem("blo_done")
        thi_done = sem("thi_done")
        tlo_done = sem("tlo_done")
        xt_done = sem("xt_done")
        xhi_done = sem("xhi_done")
        xlo_done = sem("xlo_done")
        s_mm = sem("s_mm")
        s_copied = sem("s_copied")
        shi_done = sem("shi_done")
        slo_done = sem("slo_done")
        y_mm = sem("y_mm")
        y_masked = sem("y_masked")
        z_mm = sem("z_mm")
        top_done = sem("top_done")
        rank_done = sem("rank_done")
        best_done = sem("best_done")
        gate_done = sem("gate_done")
        wh_done = sem("wh_done")
        wh_turned = sem("wh_turned")
        whi_done = sem("whi_done")
        wlo_done = sem("wlo_done")
        up_mm = sem("up_mm")
        added = sem("added")

        block = ctx.enter_context(nc.Block())

        class Head:
            def __init__(self, q, k, d):
                self.n = q * 4 + (k + d)
                self.half = q * 2 + (k + d) // 2
                self.quarter = q + (k + d) // 4
                self.s2 = (k + d) % 2
                self.s4 = (k + d) % 4
                self.there = not isinstance(q, int) or 0 <= self.n < H

        def need(eng, s, count):
            if not isinstance(count, int) or count > 0:
                eng.wait_ge(s, count)

        def run_steps(eng, step, first=-4, last=H):
            for i in range(first, 4):
                step(lambda d, i=i: Head(i // 4, i % 4, d))
            with eng.Fori(1, H // 4 - 1) as q:
                for k in range(4):
                    step(lambda d, k=k: Head(q, k, d))
            for i in range(H - 4, last + 1):
                step(lambda d, i=i: Head(i // 4, i % 4, d))

        def col(t, h):
            return t[:, bass.ds(h.n, 1)]

        def eo(t, j):
            return t[:, j, :]

        @block.sync
        def _(sp):
            sp.dma_start(logs[:, 0:N], log_A_real).then_inc(in_par, 16)
            with nc.allow_non_contiguous_dma(reason="64 numbers"):
                sp.dma_start(logs[:, N:N + 1], log_dt.rearrange("(h a) -> h a", a=1)).then_inc(in_par, 16)
            sp.dma_start(A_im[:, :], A_imag).then_inc(in_par, 16)
            sp.dma_start(C_nat[:, :, :], Cw).then_inc(in_par, 16)
            sp.dma_start(lens_i[:, :], lens.partition_broadcast(P)).then_inc(in_len, 16)
            sp.dma_start(Drow[:, :], D.rearrange("(a h) -> a h", a=1)).then_inc(in_D, 16)
            sp.dma_start(A_nat[:, :], Aw.rearrange("e r d -> (e r) d")).then_inc(in_A, 16)
            sp.dma_start(route_nat[:, :], route_w).then_inc(in_rw, 16)
            sp.wait_ge(zero_row, 1)
            for s in range(2):
                sp.dma_start(kdram[s:s + 1, Q:Q + P], zeros[:, :]).then_inc(pad_done, 16)
            sp.wait_ge(pad_done, 32)

            def head_rows(t, h):
                return bass.AP(t.tensor, h.n * L, [[H * L, P], [1, L]])

            def step(head):
                h = head(2)
                if h.there:
                    need(sp, added, (h.n - 3) * 2)
                    sp.dma_start(xt[h.s4][:, :], head_rows(x, h)).then_inc(x_in[h.s4], 16)
                    need(sp, thi_done, h.n - 1)
                    need(sp, tlo_done, h.n - 1)
                    need(sp, krow_done, h.n * 2 + 2)
                    sp.dma_start(kdram[h.s2:h.s2 + 1, 0:Q], krow[h.s2][:, :]).then_inc(k_out[h.s2], 16)
                    need(sp, k_out[h.s2], h.half * 16 + 16)
                    sp.dma_start(Traw[h.s2][:, :],
                                 bass.AP(kdram.tensor, h.s2 * (P + Q), [[1, P], [1, Q]])
                                 ).then_inc(t_in[h.s2], 16)
                h = head(-1)
                if h.there:
                    need(sp, added, h.n * 2 + 2)
                    sp.dma_start(head_rows(out, h), ost[h.s2][:, :]).then_inc(o_out[h.s2], 16)

            run_steps(sp, step)
            for s in range(2):
                sp.wait_ge(o_out[s], 16 * (H // 2))
                sp.wait_ge(t_in[s], 16 * (H // 2))

        @block.gpsimd
        def _(pool):
            pool.memset(zeros[:, :], 0.0).then_inc(zero_row, 1)
            pool.memset(ident[:, :], 0.0).then_inc(consts, 1)
            pool.memset(swap[:, :], 0.0).then_inc(consts, 1)
            pool.iota(egrid[:, :], pattern=[[-1, Q]], base=Q - 1, channel_multiplier=0,
                      allow_small_or_imprecise_dtypes=True).then_inc(consts, 1)
            pool.iota(grid16[:, :], pattern=[[-1, G16]], base=G16 - 1, channel_multiplier=0,
                      allow_small_or_imprecise_dtypes=True).then_inc(consts, 1)
            pool.iota(desc[:, :], pattern=[[-1, E]], base=E, channel_multiplier=0,
                      allow_small_or_imprecise_dtypes=True).then_inc(consts, 1)
            pool.iota(posn[:, :], pattern=[[P, NB]], base=0, channel_multiplier=1,
                      allow_small_or_imprecise_dtypes=True).then_inc(consts, 1)
            pool.wait_ge(consts, 6)
            pool.affine_select(out=ident[:, :], in_=ident[:, :], compare_op=ALU.not_equal, fill=1.0,
                               base=0, pattern=[[-1, P]], channel_multiplier=1).then_inc(consts, 1)
            pool.affine_select(out=swap[:, :], in_=swap[:, :], compare_op=ALU.not_equal, fill=1.0,
                               base=N, pattern=[[-1, P]], channel_multiplier=1).then_inc(consts, 1)
            pool.wait_ge(consts, 8)
            pool.affine_select(out=swap[:, :], in_=swap[:, :], compare_op=ALU.not_equal, fill=1.0,
                               base=-N, pattern=[[-1, P]], channel_multiplier=1).then_inc(consts, 1)
            pool.wait_ge(mag_done, 2)

            def step(head):
                h = head(3)
                if h.there:
                    need(pool, wave_done, h.n + 1)
                    need(pool, grev_done, h.n)
                    pool.tensor_tensor(
                        wave1[:, :].rearrange("p (a b) -> p a b", b=G16),
                        wave[h.s2][:, :].rearrange("p (a b) -> p a b", b=G16),
                        magP[:, bass.ds(h.n, 1), :].rearrange("p a (b c) -> p (a b) c", c=1)
                        .to_broadcast([P, G16, G16]), ALU.mult).then_inc(wave1_done, 1)
                    need(pool, wave1_done, h.n + 1)
                    need(pool, kmm_done, (h.n - 1) * 2)
                    need(pool, ghi_done, h.n - 1)
                    need(pool, glo_done, h.n - 1)
                    pool.tensor_tensor(
                        Grev[h.s2][:, :].rearrange("p (a b) -> p a b", b=G16),
                        wave1[:, :].rearrange("p (a b) -> p a b", b=G16),
                        magQ[:, bass.ds(h.n, 1), :].to_broadcast([P, G16, G16]),
                        ALU.mult).then_inc(grev_done, 1)
                h = head(0)
                if h.there:
                    need(pool, shi_done, h.n + 1)
                    need(pool, y_mm, (h.n - 1) * 2)
                    pool.tensor_tensor(Slo[h.s2][:, :], Sf[h.s2][:, :], Shi[h.s2][:, :].bitcast(F32),
                                       ALU.subtract).then_inc(slo_done, 1)
                h = head(3)
                if h.there:
                    need(pool, ghi_done, h.n + 1)
                    need(pool, y_mm, (h.n - 3) * 2)
                    pool.tensor_tensor(Glo[h.s4][:, :], Grev[h.s2][:, ::-1], Ghi[h.s4][:, :].bitcast(F32),
                                       ALU.subtract).then_inc(glo_done, 1)
                    need(pool, m1_done, h.n * 2 + 2)
                    need(pool, kmm_done, (h.n - 1) * 2)
                    pool.tensor_tensor(Mx[h.s2][:, :], m1[h.s2][:, 0, :], m1[h.s2][:, 1, :],
                                       ALU.add).then_inc(mx_done, 1)
                h = head(1)
                if h.there:
                    need(pool, r1_done, h.n * 2 + 2)
                    need(pool, s_mm, (h.n - 1) * 3)
                    pool.tensor_tensor(Rx[h.s2][:, :], r1[h.s2][:, 0, :], r1[h.s2][:, 1, :],
                                       ALU.add).then_inc(rx_done, 1)
                    need(pool, thi_done, h.n + 1)
                    need(pool, y_mm, (h.n - 1) * 2)
                    pool.tensor_tensor(Tlo[h.s2][:, :, :].rearrange("p a b -> p (a b)"), Traw[h.s2][:, ::-1],
                                       Thi[h.s2][:, :, :].rearrange("p a b -> p (a b)").bitcast(F32),
                                       ALU.subtract).then_inc(tlo_done, 1)

            run_steps(pool, step)

        @block.scalar
        def _(act):
            with nc.allow_non_contiguous_dma(reason="expert rows of 16"):
                for e in range(E):
                    act.dma_start(B_nat[:, :, e * R:(e + 1) * R],
                                  Bw[e].rearrange("(j p) r -> p j r", p=P)).then_inc(in_B, 16)
            act.wait_ge(phases_done, 1)
            act.activation(sine[:, :, :], phase[:, :, :], ACT.Sin, scale=TURN).then_inc(sines_done, 1)
            act.activation(sine_half[:, :, :], phase[:, :, :], ACT.Sin, scale=TURN / 2).then_inc(sines_done, 1)
            act.wait_ge(w_turned, 1)
            act.activation(Wt[:, 0:4, E:NW], psO[0][:, :].rearrange("p (c w) -> p c w", w=P),
                           ACT.Copy).then_inc(w_done, 1)
            act.activation(Wt[:, 4:8, E:NW], psO[1][:, :].rearrange("p (c w) -> p c w", w=P),
                           ACT.Copy).then_inc(w_done, 1)
            act.activation(Wt[:, :, 0:E], psZ[:, 0:NB * E].rearrange("p (c w) -> p c w", w=E),
                           ACT.Copy).then_inc(w_done, 1)
            for j in range(2):
                act.wait_ge(b_turned, j + 1)
                act.activation(Bw_hi[:, j * 512:(j + 1) * 512], psX[j][:, :], ACT.Copy).then_inc(bhi_set, 1)
            act.wait_ge(tabs_turned, 1)
            act.activation(tab[:, 0:8, :], psY[0][:, :].rearrange("p (t h) -> p t h", h=H),
                           ACT.Copy).then_inc(tab_done, 1)
            act.activation(tab[:, 8, :], psY[1][:, 0:H], ACT.Copy).then_inc(tab_done, 1)
            act.wait_ge(rho_done, 1)
            act.activation(magP[:, :, :], rho16[:, :, :], ACT.Exp, scale=float(G16)).then_inc(mag_done, 1)
            act.activation(magQ[:, :, :], rho16[:, :, :], ACT.Exp).then_inc(mag_done, 1)
            act.wait_ge(ck_done, 1)
            act.wait_ge(in_D, 16)
            act.wait_ge(cols_set, 8)
            act.wait_ge(consts, 9)

            def x_hi(h, j):
                need(act, xt_done, h.n * 2 + j + 1)
                need(act, y_mm, (h.n - 1) * 2)
                act.activation(eo(Xhi[h.s2], j), psX[j][:, :], ACT.Copy).then_inc(xhi_done, 1)

            def state(h, j):
                need(act, s_mm, h.n * 3 + j + 1)
                if j == 0:
                    need(act, shi_done, h.n - 1)
                    need(act, slo_done, h.n - 1)
                act.activation(Sf[h.s2][:, j * P:(j + 1) * P], psS[:, j * P:(j + 1) * P],
                               ACT.Copy).then_inc(s_copied, 1)

            def step(head):
                h = head(0)
                if h.there:
                    state(h, 0)
                h = head(1)
                if h.there:
                    x_hi(h, 0)
                h = head(0)
                if h.there:
                    state(h, 1)
                h = head(3)
                if h.there:
                    need(act, frac_done, h.n + 1)
                    need(act, wave1_done, h.n - 1)
                    act.activation(wave[h.s2][:, :], frac[h.s2][:, :], ACT.Sin, scale=TURN,
                                   bias=sinbias[:, :]).then_inc(wave_done, 1)
                h = head(0)
                if h.there:
                    state(h, 2)
                    need(act, s_copied, h.n * 3 + 3)
                    need(act, y_mm, (h.n - 1) * 2)
                    act.activation(Shi[h.s2][:, :], Sf[h.s2][:, :], ACT.Copy).then_inc(shi_done, 1)
                h = head(3)
                if h.there:
                    need(act, mx_done, h.n - 1)
                    act.activation(m1[h.s2][:, 0, :], ident[:, :], ACT.Copy,
                                   scale=col(tab[:, AM, :], h)).then_inc(m1_done, 1)
                    act.activation(m1[h.s2][:, 1, :], swap[:, :], ACT.Copy,
                                   scale=col(tab[:, BM, :], h)).then_inc(m1_done, 1)
                h = head(1)
                if h.there:
                    need(act, t_in[h.s2], h.half * 16 + 16)
                    need(act, y_mm, (h.n - 1) * 2)
                    act.activation(Thi[h.s2][:, :, :].rearrange("p a b -> p (a b)"), Traw[h.s2][:, ::-1],
                                   ACT.Copy).then_inc(thi_done, 1)
                    need(act, rx_done, h.n - 1)
                    act.activation(r1[h.s2][:, 0, :], ident[:, :], ACT.Copy,
                                   scale=col(tab[:, LR, :], h)).then_inc(r1_done, 1)
                    act.activation(r1[h.s2][:, 1, :], swap[:, :], ACT.Copy,
                                   scale=col(tab[:, BR, :], h)).then_inc(r1_done, 1)
                h = head(2)
                if h.there:
                    need(act, kmm_done, h.n * 2 + 2)
                    need(act, k_out[h.s2], h.half * 16)
                    act.activation(krow[h.s2][0:1, Q - 1:Q], psK[:, 0:1], ACT.Identity,
                                   bias=Drow[0:1, bass.ds(h.n, 1)]).then_inc(krow_done, 1)
                    act.activation(krow[h.s2][0:1, 0:Q - 1], psK[:, Q - 1:0:-1], ACT.Copy).then_inc(krow_done, 1)
                    need(act, s_mm, h.n * 3 - 5)
                    act.activation(Bhi[h.s2][:, :, :].rearrange("p a b -> p (a b)"), psB,
                                   ACT.Copy).then_inc(bhi_done, 1)
                h = head(3)
                if h.there:
                    need(act, grev_done, h.n + 1)
                    need(act, y_mm, (h.n - 3) * 2)
                    act.activation(Ghi[h.s4][:, :], Grev[h.s2][:, ::-1], ACT.Copy).then_inc(ghi_done, 1)
                    need(act, kmm_done, (h.n - 1) * 2)
                    act.activation(ck[h.s2][:, :].rearrange("p (a b) -> p a b", a=1),
                                   Ck[:, bass.ds(h.n, 1), :].bitcast(F32), ACT.Copy).then_inc(ckr_done, 1)
                h = head(1)
                if h.there:
                    x_hi(h, 1)
                h = head(-1)
                if h.there:
                    need(act, wh_turned, h.n + 1)
                    need(act, up_mm, (h.n - 1) * 2)
                    act.activation(whi[h.s2][:, :], psWh, ACT.Copy).then_inc(whi_done, 1)
                h = head(4)
                if h.there:
                    need(act, frac1_done, h.n - 1)
                    need(act, whole_done, h.n - 1)
                    act.activation(turns_h[h.s2][:, :], egrid[:, :], ACT.Copy,
                                   scale=col(tab[:, VH, :], h)).then_inc(turns_done, 1)
                    act.activation(turns_t[h.s2][:, :], egrid[:, :], ACT.Identity,
                                   scale=col(tab[:, V, :], h), bias=quarter[:, :]).then_inc(turns_done, 1)

            run_steps(act, step)

        @block.vector
        def _(dve):
            count = [0]

            def link(ins):
                count[0] += 1
                ins.then_inc(v_set, 1)
                dve.wait_ge(v_set, count[0])

            def TS(o, a, s1, s2, op0, op1=None):
                link(dve.tensor_scalar(o, a, s1, s2, op0, op1) if op1 is not None
                     else dve.tensor_scalar(o, a, s1, None, op0))

            def TT(o, a, b, op):
                link(dve.tensor_tensor(o, a, b, op))

            def STT(o, a, s, b, op0, op1):
                link(dve.scalar_tensor_tensor(o, a, s, b, op0, op1))

            def exp(o, a, w):
                v, k, r, p, t = (ex[:, j, 0:w] for j in range(5))
                TS(v, a, 88.0, -87.0, ALU.min, ALU.max)
                TS(k, v, 1.4426950408889634, ROUND, ALU.mult, ALU.add)
                TS(k, k, ROUND, None, ALU.subtract)
                STT(r, k, -0.693359375, v, ALU.mult, ALU.add)
                STT(r, k, 2.12194440e-4, r, ALU.mult, ALU.add)
                TS(p, r, 1.0 / 5040, None, ALU.mult)
                for c in (1 / 720, 1 / 120, 1 / 24, 1 / 6, 0.5, 1.0):
                    STT(p, p, c, r, ALU.add, ALU.mult)
                TS(t.bitcast(I32), k, 127.0, None, ALU.add)
                TS(t.bitcast(I32), t.bitcast(I32), 23, None, ALU.logical_shift_left)
                STT(o, p, 1.0, t, ALU.add, ALU.mult)

            for t, lo, hi in ((quarter, -0.25, 0.0), (sinbias, 1.5707962, 0.0),
                              (clamp_lo, -0.75, -0.5), (clamp_hi, 0.25, 0.5)):
                dve.memset(t[0:N, :], lo).then_inc(cols_set, 1)
                dve.memset(t[N:P, :], hi).then_inc(cols_set, 1)
            dve.wait_ge(in_par, 64)
            exp(exps[:, :], logs[:, :], N + 1)
            ar, dt, Ai = exps[:, 0:N], exps[:, N:N + 1], A_im[:, :]
            rho = pack[:, RHO, 0, :]
            TS(rho, ar, dt, -1.0, ALU.mult, ALU.mult)
            TS(w[:, :], Ai, dt, None, ALU.mult)
            inv = 1.0 / (2.0 * np.pi)
            c1 = float(np.round(inv * 2**14) / 2**14)
            c2 = float(np.round((inv - c1) * 2**27) / 2**27)
            c3 = float(inv - c1 - c2)
            link(dve.tensor_copy(w12[:, :], w[:, :]))
            w1 = w12[:, :].bitcast(F32)
            TT(w2[:, :], w[:, :], w1, ALU.subtract)
            v, vh, vl = pack[:, V, 0, :], pack[:, VH, 0, :], pack[:, VL, 0, :]
            TS(v, w[:, :], inv, None, ALU.mult)
            link(dve.tensor_copy(v12[:, :], v))
            link(dve.tensor_copy(vh, v12[:, :].bitcast(F32)))
            TS(tmp[:, 0, :], w1, c1, None, ALU.mult)
            TT(tmp[:, 0, :], tmp[:, 0, :], vh, ALU.subtract)
            STT(tmp[:, 0, :], w1, c2, tmp[:, 0, :], ALU.mult, ALU.add)
            STT(tmp[:, 0, :], w2[:, :], c1, tmp[:, 0, :], ALU.mult, ALU.add)
            STT(tmp[:, 0, :], w2[:, :], c2, tmp[:, 0, :], ALU.mult, ALU.add)
            STT(tmp[:, 0, :], w1, c3, tmp[:, 0, :], ALU.mult, ALU.add)
            TS(vl, tmp[:, 0, :], -1.0, None, ALU.mult)
            for j, e in enumerate((1.0, float(Q))):
                g, t = phase[:, j, :], tmp[:, 1, :]
                TS(t, v, e, ROUND, ALU.mult, ALU.add)
                TS(t, t, ROUND, None, ALU.subtract)
                STT(g, vh, e, t, ALU.mult, ALU.subtract)
                STT(g, tmp[:, 0, :], e, g, ALU.mult, ALU.add)
                TS(g, g, -0.5, 0.5, ALU.max, ALU.min)
            link(dve.tensor_copy(rr[:, 0:N], rho))
            dve.tensor_scalar(rr[:, N:2 * N], rho, float(Q), None, ALU.mult).then_inc(phases_done, 1)
            dve.wait_ge(phases_done, 1)
            exp(er[:, :], rr[:, :], 2 * N)
            e1, e256 = er[:, 0:N], er[:, N:2 * N]
            dve.wait_ge(sines_done, 2)
            STT(cm1[:, :, :], sine_half[:, :, :], -2.0, sine_half[:, :, :], ALU.mult, ALU.mult)
            nr, ni, Lr = (tmp[:, j, :] for j in range(2, 5))
            TT(nr, e1, cm1[:, 0, :], ALU.mult)
            STT(nr, e1, -1.0, nr, ALU.add, ALU.add)
            TT(ni, e1, sine[:, 0, :], ALU.mult)
            TS(Lr, nr, 1.0, None, ALU.add)
            STT(pack[:, LR, 0, :], cm1[:, 1, :], 1.0, e256, ALU.add, ALU.mult)
            TT(pack[:, BR, 0, :], sine[:, 1, :], e256, ALU.mult)
            den, Nr, Ni, Qr, Qi, t0 = (tmp[:, j, :] for j in range(5, 11))
            Cr, Ci = C_nat[:, :, 0], C_nat[:, :, 1]
            TT(den, ar, ar, ALU.mult)
            TT(t0, Ai, Ai, ALU.mult)
            TT(den, den, t0, ALU.add)
            link(dve.reciprocal(den, den))

            def cross(o, a, b, c, d, op):
                TT(t0, a, b, ALU.mult)
                TT(o, c, d, ALU.mult)
                TT(o, t0, o, op)

            cross(Nr, Cr, nr, Ci, ni, ALU.subtract)
            cross(Ni, Cr, ni, Ci, nr, ALU.add)
            cross(Qr, Ni, Ai, Nr, ar, ALU.subtract)
            cross(Qi, Nr, Ai, Ni, ar, ALU.add)
            zr, zi = pack[:, CK, 0, :], pack[:, CK, 1, :]
            STT(zr, Qr, 2.0, den, ALU.mult, ALU.mult)
            STT(zi, Qi, -2.0, den, ALU.mult, ALU.mult)
            cross(pack[:, AM, 0, :], zr, Lr, zi, ni, ALU.subtract)
            cross(pack[:, BM, 0, :], zr, ni, zi, Lr, ALU.add)
            link(dve.tensor_copy(pack[:, 0:6, 1, :], pack[:, 0:6, 0, :]))
            dve.tensor_scalar(pack[:, 6:8, 1, :], pack[:, 6:8, 0, :], -1.0, None,
                              ALU.mult).then_inc(pack_done, 1)
            dve.wait_ge(cols_set, 8)
            dve.wait_ge(in_len, 16)
            dve.wait_ge(consts, 9)
            link(dve.tensor_copy(lens_f[:, :], lens_i[:, :]))
            for c in range(NB):
                last = dve.tensor_scalar(mask[:, c % 2, c // 2, :], lens_f[:, :], posn[:, c:c + 1], None,
                                         ALU.is_gt)
                link(last)
            for j in range(2):
                dve.wait_ge(bhi_set, j + 1)
                dve.tensor_tensor(Bw_lo[:, j * 512:(j + 1) * 512], psX[j][:, :],
                                  Bw_hi[:, j * 512:(j + 1) * 512].bitcast(F32),
                                  ALU.subtract).then_inc(blo_set, 1)
            dve.wait_ge(tab_done, 2)
            dve.tensor_tensor(rho16[:, :, :],
                              tab[:, RHO, :].rearrange("p (h a) -> p h a", a=1).to_broadcast([P, H, G16]),
                              grid16[:, :].rearrange("p (a g) -> p a g", a=1).to_broadcast([P, H, G16]),
                              ALU.mult).then_inc(rho_done, 1)
            dve.tensor_copy(Ck[:, :, 0], tab[:, CK, :]).then_inc(ck_hi_done, 1)
            dve.wait_ge(ck_hi_done, 1)
            dve.tensor_tensor(Ck[:, :, 1], tab[:, CK, :], Ck[:, :, 0].bitcast(F32),
                              ALU.subtract).then_inc(ck_done, 1)

            def x_lo(h, j):
                need(dve, xhi_done, h.n * 2 + j + 1)
                need(dve, y_mm, (h.n - 1) * 2)
                dve.tensor_tensor(eo(Xlo[h.s2], j), psX[j][:, :], eo(Xhi[h.s2], j).bitcast(F32),
                                  ALU.subtract).then_inc(xlo_done, 1)

            def step(head):
                h = head(3)
                if h.there:
                    need(dve, turns_done, h.n * 2 + 2)
                    need(dve, frac1_done, h.n)
                    dve.tensor_scalar(whole[:, :], turns_t[h.s2][:, :], ROUND, None,
                                      ALU.add).then_inc(whole_done, 1)
                    need(dve, whole_done, h.n + 1)
                    need(dve, frac2_done, h.n)
                    dve.scalar_tensor_tensor(frac1[:, :], whole[:, :], ROUND, turns_h[h.s2][:, :],
                                             ALU.subtract, ALU.subtract).then_inc(frac1_done, 1)
                    need(dve, frac1_done, h.n + 1)
                    need(dve, frac_done, h.n)
                    dve.scalar_tensor_tensor(frac2[:, :], egrid[:, :], col(tab[:, VL, :], h), frac1[:, :],
                                             ALU.mult, ALU.add).then_inc(frac2_done, 1)
                    need(dve, frac2_done, h.n + 1)
                    need(dve, wave_done, h.n - 1)
                    dve.tensor_scalar(frac[h.s2][:, :], frac2[:, :], clamp_lo[:, :], clamp_hi[:, :],
                                      ALU.max, ALU.min).then_inc(frac_done, 1)
                h = head(1)
                if h.there:
                    x_lo(h, 0)
                h = head(-1)
                if h.there:
                    need(dve, z_mm, h.n + 1)
                    need(dve, gate_done, h.n)
                    dve.reduce_max(top[:, :], psZ[:, 0:E], axis=AX.X).then_inc(top_done, 1)
                    need(dve, top_done, h.n + 1)
                    dve.scalar_tensor_tensor(rank[:, :], psZ[:, 0:E], top[:, :], desc[:, :],
                                             ALU.is_equal, ALU.mult).then_inc(rank_done, 1)
                    need(dve, rank_done, h.n + 1)
                    dve.reduce_max(best[:, :], rank[:, :], axis=AX.X).then_inc(best_done, 1)
                    need(dve, best_done, h.n + 1)
                    need(dve, wh_done, h.n)
                    dve.tensor_scalar(gate[:, :], rank[:, :], best[:, :], top[:, :],
                                      ALU.is_equal, ALU.mult).then_inc(gate_done, 1)
                    need(dve, gate_done, h.n + 1)
                    need(dve, wh_turned, h.n)
                    dve.tensor_tensor(wh[:, :].rearrange("p (e r) -> p e r", r=R),
                                      psZ[:, E:NW].rearrange("p (e r) -> p e r", r=R),
                                      gate[:, :].rearrange("p (e a) -> p e a", a=1)
                                      .to_broadcast([P, E, R]), ALU.mult).then_inc(wh_done, 1)
                h = head(2)
                if h.there:
                    need(dve, bhi_done, h.n + 1)
                    need(dve, s_mm, h.n * 3 - 5)
                    dve.tensor_tensor(Blo[h.s2][:, :, :].rearrange("p a b -> p (a b)"), psB,
                                      Bhi[h.s2][:, :, :].rearrange("p a b -> p (a b)").bitcast(F32),
                                      ALU.subtract).then_inc(blo_done, 1)
                h = head(1)
                if h.there:
                    x_lo(h, 1)
                h = head(-1)
                if h.there:
                    need(dve, whi_done, h.n + 1)
                    need(dve, up_mm, (h.n - 1) * 2)
                    dve.tensor_tensor(wlo[h.s2][:, :], psWh, whi[h.s2][:, :].bitcast(F32),
                                      ALU.subtract).then_inc(wlo_done, 1)
                h = head(0)
                if h.there:
                    for j in range(2):
                        need(dve, y_mm, h.n * 2 + j + 1)
                        need(dve, z_mm, h.n)
                        dve.tensor_tensor(Y[:, j, :, :].rearrange("p a b -> p (a b)"), psY[j][:, :],
                                          mask[:, j, :, :].rearrange("p a b -> p (a b)"),
                                          ALU.mult).then_inc(y_masked, 1)
                h = head(-1)
                if h.there:
                    for j in range(2):
                        need(dve, up_mm, h.n * 2 + j + 1)
                        need(dve, x_in[h.s4], h.quarter * 16 + 16)
                        need(dve, o_out[h.s2], h.half * 16)
                        half = slice(j * 512, (j + 1) * 512)
                        dve.tensor_tensor(ost[h.s2][:, half], psO[j][:, :], xt[h.s4][:, half],
                                          ALU.add).then_inc(added, 1)

            run_steps(dve, step)

        @block.tensor
        def _(pe):
            pe.wait_ge(consts, 9)
            pe.wait_ge(in_A, 16)
            pe.wait_ge(in_rw, 16)
            for c in range(NB):
                cols = slice((c % 4) * P, (c % 4 + 1) * P)
                pe.transpose(psO[c // 4][:, cols], A_nat[:, c * P:(c + 1) * P], ident[:, :])
            for c in range(NB):
                last = pe.transpose(psZ[:, c * E:(c + 1) * E], route_nat[:, c * P:(c + 1) * P],
                                    ident[0:E, 0:E])
            last.then_inc(w_turned, 1)
            pe.wait_ge(pack_done, 1)
            for t in range(NT):
                last = pe.transpose(psY[t // 8][:, (t % 8) * H:(t % 8 + 1) * H],
                                    pack[:, t, :, :].rearrange("h a n -> h (a n)"), ident[0:H, 0:H])
            last.then_inc(tabs_turned, 1)
            pe.wait_ge(in_B, 16 * E)
            for c in range(NB):
                cols = slice((c % 4) * P, (c % 4 + 1) * P)
                last = pe.transpose(psX[c // 4][:, cols], B_nat[:, c, :], ident[:, :])
                if c % 4 == 3:
                    last.then_inc(b_turned, 1)
            pe.wait_ge(blo_set, 2)
            pe.wait_ge(bhi_set, 2)
            pe.wait_ge(tab_done, 2)
            pe.wait_ge(w_done, 3)

            def three(dst, pairs, first, last):
                n = 3 * len(pairs)
                i = 0
                for (ah, al), (bh, bl) in pairs:
                    for a, b in ((ah, bh), (ah, bl), (al, bh)):
                        mm = pe.matmul(dst, a, b, start=first and i == 0, stop=last and i == n - 1,
                                       skip_group_check=True)
                        i += 1
                return mm

            def turn_x(h, j):
                need(pe, x_in[h.s4], h.quarter * 16 + 16)
                need(pe, xhi_done, h.n * 2 - 1 + j)
                need(pe, xlo_done, h.n * 2 - 1 + j)
                for c in range(NE):
                    at = (2 * c + j) * P
                    last = pe.transpose(psX[j][:, c * P:(c + 1) * P], xt[h.s4][:, at:at + P], ident[:, :])
                last.then_inc(xt_done, 1)

            def project(h, j):
                need(pe, y_masked, h.n * 2 + j + 1)
                if j == 0:
                    need(pe, wlo_done, h.n)
                for c in range(NE):
                    last = pe.matmul(psZ[:, 0:NW], Y[:, j, c, :], Wt[:, 2 * c + j, :],
                                     start=(j == 0 and c == 0), stop=(j == 1 and c == NE - 1),
                                     skip_group_check=True)
                if j == 1:
                    last.then_inc(z_mm, 1)

            def carry(h, j):
                need(pe, s_copied, h.n * 3 + j + 1)
                need(pe, rx_done, h.n + 1)
                pe.matmul(psS[:, (j + 1) * P:(j + 2) * P], Rx[h.s2][:, :], Sf[h.s2][:, j * P:(j + 1) * P],
                          start=False, stop=(j == NS - 2), skip_group_check=True).then_inc(s_mm, 1)

            def step(head):
                h = head(0)
                if h.there:
                    need(pe, xhi_done, h.n * 2 + 2)
                    need(pe, xlo_done, h.n * 2 + 2)
                    need(pe, bhi_done, h.n + 1)
                    need(pe, blo_done, h.n + 1)
                    need(pe, s_copied, h.n * 3)
                    w = NS * P
                    three(psS[:, 0:w],
                          [((Bhi[h.s2][:, j, :], Blo[h.s2][:, j, :]), (Xhi[h.s2][:, j, 0:w], Xlo[h.s2][:, j, 0:w]))
                           for j in range(2)], True, False).then_inc(s_mm, 1)
                h = head(1)
                if h.there:
                    turn_x(h, 0)
                h = head(0)
                if h.there:
                    carry(h, 0)
                h = head(-1)
                if h.there:
                    project(h, 0)
                h = head(0)
                if h.there:
                    carry(h, 1)
                h = head(-1)
                if h.there:
                    project(h, 1)
                h = head(2)
                if h.there:
                    need(pe, ghi_done, h.n + 1)
                    need(pe, glo_done, h.n + 1)
                    need(pe, ckr_done, h.n + 1)
                    need(pe, added, (h.n - 3) * 2 - 1)
                    need(pe, blo_done, h.n)
                    three(psK, [((ck[h.s2][:, 0:1], ck[h.s2][:, 1:2]), (Ghi[h.s4][:, :], Glo[h.s4][:, :]))],
                          True, True).then_inc(kmm_done, 1)
                    need(pe, mx_done, h.n + 1)
                    need(pe, grev_done, h.n + 1)
                    for j in range(2):
                        last = pe.matmul(psB[:, j * P:(j + 1) * P], Grev[h.s2][:, j * P:(j + 1) * P],
                                         Mx[h.s2][:, :], start=True, stop=True, skip_group_check=True)
                    last.then_inc(kmm_done, 1)
                h = head(0)
                if h.there:
                    need(pe, thi_done, h.n + 1)
                    need(pe, tlo_done, h.n + 1)
                    T = [(Thi[h.s2][:, j, :], Tlo[h.s2][:, j, :]) for j in range(2)]
                    X = [(Xhi[h.s2][:, j, :], Xlo[h.s2][:, j, :]) for j in range(2)]
                    need(pe, y_masked, h.n * 2 - 1)
                    three(psY[0][:, :], [(T[0], X[0])], True, False)
                    need(pe, y_masked, h.n * 2)
                    three(psY[1][:, :], [(T[0], X[1]), (T[1], X[0])], True, False)
                h = head(1)
                if h.there:
                    turn_x(h, 1)
                h = head(-1)
                if h.there:
                    need(pe, wh_done, h.n + 1)
                    need(pe, whi_done, h.n)
                    need(pe, wlo_done, h.n)
                    pe.transpose(psWh, wh[:, :], ident[:, :]).then_inc(wh_turned, 1)
                h = head(0)
                if h.there:
                    need(pe, shi_done, h.n + 1)
                    need(pe, slo_done, h.n + 1)
                    for j in range(2):
                        G = tuple(g[h.s4][:, j * P:(j + 1) * P] for g in (Ghi, Glo))
                        three(psY[j][:, P:512], [(G, (Shi[h.s2][:, :], Slo[h.s2][:, :]))],
                              False, True).then_inc(y_mm, 1)
                h = head(-1)
                if h.there:
                    need(pe, whi_done, h.n + 1)
                    need(pe, wlo_done, h.n + 1)
                    ahead = head(2)
                    if ahead.there:
                        need(pe, krow_done, ahead.n * 2 + 2)
                        need(pe, bhi_done, ahead.n + 1)
                        need(pe, blo_done, ahead.n + 1)
                    for j in range(2):
                        need(pe, added, h.n * 2 - 1 + j)
                        half = slice(j * 512, (j + 1) * 512)
                        three(psO[j][:, :], [((whi[h.s2][:, :], wlo[h.s2][:, :]),
                                              (Bw_hi[:, half], Bw_lo[:, half]))],
                              True, True).then_inc(up_mm, 1)

            run_steps(pe, step)


_INS = ['x', 'itok_B_8_3872', 'L0_cond_log_dt', 'L0_cond_C', 'L0_cond_log_A_real', 'L0_cond_A_imag',
        'L0_cond_D', 'L0_ffn_route_w', 'L0_ffn_A', 'L0_ffn_Bw']


def kernel(**inputs):
    import numpy as _np
    import concourse.bacc as _bacc
    from concourse import mybir as _mybir
    from concourse.bass_utils import run_bass_kernel_spmd as _run

    nc = _bacc.Bacc("TRN2", target_bir_lowering=False, num_devices=1)
    arrays, args = {}, []
    for name in _INS:
        a = _np.ascontiguousarray(inputs[name])
        arrays[f"in_{name}_dram"] = a
        args.append(nc.dram_tensor(f"in_{name}_dram", a.shape, _mybir.dt.from_np(a.dtype), kind="ExternalInput").ap())
    shape = inputs['x'].shape
    args.append(nc.dram_tensor("out_0_dram", shape, _mybir.dt.float32, kind="ExternalOutput").ap())
    conv_ffn_kernel(nc, *args)
    r = _run(nc, [arrays], core_ids=[0])
    return r.results[0]["out_0_dram"]
```

```python
import concourse.bass as bass
import numpy as np
from concourse import mybir
from contextlib import ExitStack


F32 = mybir.dt.float32
F32R = mybir.dt.float32r
I32 = mybir.dt.int32
ALU = mybir.AluOpType
ACT = mybir.ActivationFunctionType
AX = mybir.AxisListType

P = 128
ROUND = 12582912.0
TURN = 6.283185


def conv_ffn_kernel(nc, x, lens, log_dt, Cw, log_A_real, A_imag, D, route_w, Aw, Bw, out):
    B, H, L = x.shape
    N = A_imag.shape[1]
    E, R, _ = Aw.shape
    ER = E * R
    NB = L // P
    NE = NB // 2
    Q = 2 * P
    NS = NE - 1
    NW = ER + E
    HALF = L // 2
    G16 = 16
    assert B == P and 2 * N == P and ER == P and HALF == 512 and H % 4 == 0

    ctx = ExitStack()
    with ctx:
        def sb(name, shape, dt=F32):
            return ctx.enter_context(nc.sbuf_tensor(name, shape, dt))

        def bank(name):
            return ctx.enter_context(nc.psum_tensor(name, [P, 512], F32))

        def sem(name):
            return ctx.enter_context(nc.semaphore(name))

        ident = sb("ident", [P, P])
        swap = sb("swap", [P, P])
        egrid = sb("egrid", [P, Q])
        grid16 = sb("grid16", [P, G16])
        desc = sb("desc", [P, E])
        quarter = sb("quarter", [P, 1])
        posn = sb("posn", [P, NB])
        lens_i = sb("lens_i", [P, P], I32)
        lens_f = sb("lens_f", [P, P])
        mask = sb("mask", [P, 2, NE, P])
        zeros = sb("zeros", [1, P])
        Dcol = sb("Dcol", [P, H])
        route_nat = sb("route_nat", [E, L])
        A_nat = sb("A_nat", [P, L])
        B_nat = sb("B_nat", [P, NB, ER])
        Wt = sb("Wt", [P, NB, NW])
        Bw_hi = sb("Bw_hi", [P, L], F32R)
        Bw_lo = sb("Bw_lo", [P, L], F32R)
        logs = sb("logs", [H, N + 1])
        A_im = sb("A_im", [H, N])
        C_nat = sb("C_nat", [H, N, 2])
        V, VH, VL, RHO = range(4)
        LR, BM, AM, BR, CK = range(5)
        pack1 = sb("pack1", [H, 4, 2, N])
        pack2 = sb("pack2", [H, 5, 2, N])
        tab1 = sb("tab1", [P, 4, H])
        tab2 = sb("tab2", [P, 5, H])
        FIRST_HEADS = 8
        MAG_PARTS = [slice(0, FIRST_HEADS), slice(FIRST_HEADS, H)]
        rho16 = sb("rho16", [P, H, G16])
        magP = sb("magP", [P, H, G16])
        magQ = sb("magQ", [P, H, G16])
        ex = sb("ex", [H, 5, 2 * N])
        exps = sb("exps", [H, N + 1])
        w = sb("w", [H, N])
        w12 = sb("w12", [H, N], F32R)
        w2 = sb("w2", [H, N])
        v12 = sb("v12", [H, N], F32R)
        tmp = sb("tmp", [H, 2, N])
        err = sb("err", [H, N])
        ptmp = sb("ptmp", [H, N])
        pair = sb("pair", [H, 2, 2, N])
        prod = sb("prod", [H, 2, 2, N])
        CL = sb("CL", [H, 2, N])
        QQ = sb("QQ", [H, 2, N])
        phase = sb("phase", [H, 2, N])
        rr = sb("rr", [H, 2 * N])
        er = sb("er", [H, 2 * N])
        sine = sb("sine", [H, 2, N])
        sine_half = sb("sine_half", [H, 2, N])
        cm1 = sb("cm1", [H, 2, N])
        xt = [sb(f"xt{s}", [P, L]) for s in range(4)]
        Xhi = [sb(f"Xhi{s}", [P, 2, HALF], F32R) for s in range(2)]
        Xlo = [sb(f"Xlo{s}", [P, 2, HALF], F32R) for s in range(2)]
        turns_h = [sb(f"turns_h{s}", [P, Q]) for s in range(2)]
        turns_t = [sb(f"turns_t{s}", [P, Q]) for s in range(2)]
        whole = [sb(f"whole{s}", [P, Q]) for s in range(2)]
        frac1 = [sb(f"frac1_{s}", [P, Q]) for s in range(2)]
        frac2 = sb("frac2", [P, Q])
        fraction = [sb(f"fraction{s}", [P, Q]) for s in range(2)]
        wave = [sb(f"wave_{s}", [P, Q]) for s in range(2)]
        wave1 = sb("wave1", [P, Q])
        Grev = [sb(f"Grev{s}", [P, Q]) for s in range(2)]
        Ghi = [sb(f"Ghi{s}", [P, Q], F32R) for s in range(4)]
        Glo = [sb(f"Glo{s}", [P, Q], F32R) for s in range(4)]
        m1 = [sb(f"m1_{s}", [P, 2, P]) for s in range(2)]
        Mx = [sb(f"Mx{s}", [P, P + 1]) for s in range(2)]
        kcol = [sb(f"kcol{s}", [P, 2]) for s in range(2)]
        Bhi = [sb(f"Bhi{s}", [P, 2, P], F32R) for s in range(2)]
        Blo = [sb(f"Blo{s}", [P, 2, P], F32R) for s in range(2)]
        Traw = [sb(f"Traw{s}", [P, Q]) for s in range(2)]
        Thi = [sb(f"Thi{s}", [P, 2, P], F32R) for s in range(2)]
        Tlo = [sb(f"Tlo{s}", [P, 2, P], F32R) for s in range(2)]
        Sf = [sb(f"Sf{s}", [P, NS * P]) for s in range(2)]
        brought = sb("brought", [P, P])
        Shi = [sb(f"Shi{s}", [P, NS * P], F32R) for s in range(2)]
        Slo = [sb(f"Slo{s}", [P, NS * P], F32R) for s in range(2)]
        Y = sb("Y", [P, 2, NE, P])
        top = sb("top", [P, 1])
        rank = sb("rank", [P, E])
        best = sb("best", [P, 1])
        gate = sb("gate", [P, E])
        wh = sb("wh", [P, ER])
        whi = [sb(f"whi{s}", [P, P], F32R) for s in range(2)]
        wlo = [sb(f"wlo{s}", [P, P], F32R) for s in range(2)]
        ost = [sb(f"ost{s}", [P, L]) for s in range(2)]

        kdram = nc.dram_tensor("kdram", [2, P + Q], F32, kind="Internal").ap()

        psX = [bank("psXe"), bank("psXo")]
        psY = [bank("psYe"), bank("psYo")]
        psS = bank("psS")
        psZ = bank("psZ")
        psO = [bank("psO0"), bank("psO1")]
        psB = psO[0][:, :].rearrange("p (j w) -> p j w", j=2)[:, :, 0:P + 1]
        psWh = psZ[:, 256:256 + P]

        in_logs = sem("in_logs")
        in_par = sem("in_par")
        in_len = sem("in_len")
        in_D = sem("in_D")
        in_rw = sem("in_rw")
        in_A = sem("in_A")
        in_B = sem("in_B")
        pad_done = sem("pad_done")
        consts = sem("consts")
        cols_set = sem("cols_set")
        zero_row = sem("zero_row")
        v_set = sem("v_set")
        phases_done = sem("phases_done")
        sines_done = sem("sines_done")
        pack1_done = sem("pack1_done")
        pack2_done = sem("pack2_done")
        w_set = sem("w_set")
        g_set = sem("g_set")
        tabs_turned = sem("tabs_turned")
        tab_done = sem("tab_done")
        rho_done = sem("rho_done")
        mag_done = sem("mag_done")
        mask_done = sem("mask_done")
        w_turned = sem("w_turned")
        w_done = sem("w_done")
        b_turned = sem("b_turned")
        bhi_set = sem("bhi_set")
        blo_set = sem("blo_set")
        x_in = [sem(f"x_in{s}") for s in range(4)]
        k_out = [sem(f"k_out{s}") for s in range(2)]
        t_in = [sem(f"t_in{s}") for s in range(2)]
        o_out = [sem(f"o_out{s}") for s in range(2)]
        turns_done = sem("turns_done")
        whole_done = sem("whole_done")
        frac1_done = sem("frac1_done")
        frac2_done = sem("frac2_done")
        frac_done = sem("frac_done")
        wave_done = sem("wave_done")
        wave1_done = sem("wave1_done")
        grev_done = sem("grev_done")
        ghi_done = sem("ghi_done")
        glo_done = sem("glo_done")
        m1_done = sem("m1_done")
        mx_done = sem("mx_done")
        kw_done = sem("kw_done")
        b_mm = sem("b_mm")
        kcol_done = sem("kcol_done")
        bhi_done = sem("bhi_done")
        blo_done = sem("blo_done")
        thi_done = sem("thi_done")
        tlo_done = sem("tlo_done")
        xt_done = sem("xt_done")
        xhi_done = sem("xhi_done")
        xlo_done = sem("xlo_done")
        s_mm = sem("s_mm")
        s0_copied = sem("s0_copied")
        brought_done = sem("brought_done")
        s_carried = sem("s_carried")
        shi_done = sem("shi_done")
        slo_done = sem("slo_done")
        y_mm = sem("y_mm")
        y_masked = sem("y_masked")
        z_mm = sem("z_mm")
        top_done = sem("top_done")
        rank_done = sem("rank_done")
        best_done = sem("best_done")
        gate_done = sem("gate_done")
        wh_done = sem("wh_done")
        wh_turned = sem("wh_turned")
        whi_done = sem("whi_done")
        wlo_done = sem("wlo_done")
        up_mm = sem("up_mm")
        added = sem("added")

        block = ctx.enter_context(nc.Block())

        class Head:
            def __init__(self, q, k, d):
                self.n = q * 4 + (k + d)
                self.half = q * 2 + (k + d) // 2
                self.quarter = q + (k + d) // 4
                self.s2 = (k + d) % 2
                self.s4 = (k + d) % 4
                self.there = not isinstance(q, int) or 0 <= self.n < H

        def need(eng, s, count):
            if not isinstance(count, int) or count > 0:
                eng.wait_ge(s, count)

        def run_steps(eng, step):
            for i in range(4):
                step(lambda d, i=i: Head(0, i, d))
            with eng.Fori(1, H // 4 - 1) as q:
                for k in range(4):
                    step(lambda d, k=k: Head(q, k, d))
            for i in range(H - 4, H + 1):
                step(lambda d, i=i: Head(i // 4, i % 4, d))

        def col(t, h):
            return t[:, bass.ds(h.n, 1)]

        def eo(t, j):
            return t[:, j, :]

        @block.sync
        def _(sp):
            sp.dma_start(logs[:, 0:N], log_A_real).then_inc(in_logs, 16)
            sp.dma_start(A_im[:, :], A_imag).then_inc(in_par, 16)
            sp.dma_start(C_nat[:, :, :], Cw).then_inc(in_par, 16)
            sp.dma_start(lens_i[:, :], lens.partition_broadcast(P)).then_inc(in_len, 16)
            sp.dma_start(A_nat[:, :], Aw.rearrange("e r d -> (e r) d")).then_inc(in_A, 16)
            sp.dma_start(route_nat[:, :], route_w).then_inc(in_rw, 16)
            sp.wait_ge(zero_row, 2)
            sp.dma_start(Dcol[P - 1:P, :], D.rearrange("(a h) -> a h", a=1)).then_inc(in_D, 16)
            for s in range(2):
                sp.dma_start(kdram[s:s + 1, Q:Q + P], zeros[:, :]).then_inc(pad_done, 16)
            sp.wait_ge(pad_done, 32)

            def head_rows(t, h):
                return bass.AP(t.tensor, h.n * L, [[H * L, P], [1, L]])

            def load_x(h):
                need(sp, added, (h.n - 3) * 2)
                sp.dma_start(xt[h.s4][:, :], head_rows(x, h)).then_inc(x_in[h.s4], 16)

            def turn_kernel(h):
                need(sp, thi_done, h.n - 1)
                need(sp, tlo_done, h.n - 1)
                need(sp, kcol_done, h.n * 2 + 2)
                with nc.allow_non_contiguous_dma(reason="a column of numbers"):
                    sp.dma_start(bass.AP(kdram.tensor, h.s2 * (P + Q), [[1, P], [P, 2], [1, 1]]),
                                 kcol[h.s2][:, :].rearrange("p (j a) -> p j a", a=1)).then_inc(k_out[h.s2], 16)
                need(sp, k_out[h.s2], h.half * 16 + 16)
                sp.dma_start(Traw[h.s2][:, :],
                             bass.AP(kdram.tensor, h.s2 * (P + Q), [[1, P], [1, Q]])
                             ).then_inc(t_in[h.s2], 16)

            def store(h):
                need(sp, added, h.n * 2 + 2)
                sp.dma_start(head_rows(out, h), ost[h.s2][:, :]).then_inc(o_out[h.s2], 16)

            def step(head):
                if head(2).there:
                    load_x(head(2))
                    turn_kernel(head(2))
                if head(-1).there:
                    store(head(-1))

            for n in range(2):
                load_x(Head(0, n, 0))
            for n in range(2):
                turn_kernel(Head(0, n, 0))
            run_steps(sp, step)
            for s in range(2):
                sp.wait_ge(o_out[s], 16 * (H // 2))
                sp.wait_ge(t_in[s], 16 * (H // 2))

        @block.gpsimd
        def _(pool):
            pool.memset(zeros[:, :], 0.0).then_inc(zero_row, 1)
            pool.memset(Dcol[:, :], 0.0).then_inc(zero_row, 1)
            pool.memset(ident[:, :], 0.0).then_inc(consts, 1)
            pool.memset(swap[:, :], 0.0).then_inc(consts, 1)
            pool.iota(egrid[:, :], pattern=[[-1, Q]], base=Q - 1, channel_multiplier=0,
                      allow_small_or_imprecise_dtypes=True).then_inc(consts, 1)
            pool.iota(grid16[:, :], pattern=[[-1, G16]], base=G16 - 1, channel_multiplier=0,
                      allow_small_or_imprecise_dtypes=True).then_inc(consts, 1)
            pool.iota(desc[:, :], pattern=[[-1, E]], base=E, channel_multiplier=0,
                      allow_small_or_imprecise_dtypes=True).then_inc(consts, 1)
            pool.iota(posn[:, :], pattern=[[P, NB]], base=0, channel_multiplier=1,
                      allow_small_or_imprecise_dtypes=True).then_inc(consts, 1)
            pool.wait_ge(consts, 6)
            pool.affine_select(out=ident[:, :], in_=ident[:, :], compare_op=ALU.not_equal, fill=1.0,
                               base=0, pattern=[[-1, P]], channel_multiplier=1).then_inc(consts, 1)
            pool.affine_select(out=swap[:, :], in_=swap[:, :], compare_op=ALU.not_equal, fill=1.0,
                               base=N, pattern=[[-1, P]], channel_multiplier=1).then_inc(consts, 1)
            pool.wait_ge(consts, 8)
            pool.affine_select(out=swap[:, :], in_=swap[:, :], compare_op=ALU.not_equal, fill=1.0,
                               base=-N, pattern=[[-1, P]], channel_multiplier=1).then_inc(consts, 1)

            def chain(ins, n=[0]):
                n[0] += 1
                ins.then_inc(g_set, 1)
                pool.wait_ge(g_set, n[0])

            pool.wait_ge(pack1_done, 1)
            v, vh, vln = (pack1[:, t, 0, :] for t in (V, VH, VL))
            for j, e in enumerate((1.0, float(Q))):
                g, t = phase[:, j, :], ptmp[:, :]
                chain(pool.tensor_scalar(t, v, e, ROUND, ALU.mult, ALU.add))
                chain(pool.tensor_scalar(t, t, 1.0, -ROUND, ALU.mult, ALU.add))
                chain(pool.tensor_scalar(g, vh, e, 0.0, ALU.mult, ALU.add))
                chain(pool.tensor_tensor(g, g, t, ALU.subtract))
                chain(pool.tensor_scalar(t, vln, e, 0.0, ALU.mult, ALU.add))
                chain(pool.tensor_tensor(g, g, t, ALU.subtract))
                pool.tensor_scalar(g, g, 0.5, -0.5, ALU.min, ALU.max).then_inc(phases_done, 1)

            def turn_parts(h):
                need(pool, whole_done, h.n + 1)
                need(pool, frac2_done, h.n - 1)
                pool.tensor_tensor(frac1[h.s2][:, :], whole[h.s2][:, :], turns_h[h.s2][:, :],
                                   ALU.subtract).then_inc(frac1_done, 1)

            def g_table(h):
                need(pool, wave_done, h.n + 1)
                need(pool, grev_done, h.n)
                pool.tensor_tensor(
                    wave1[:, :].rearrange("p (a b) -> p a b", b=G16),
                    wave[h.s2][:, :].rearrange("p (a b) -> p a b", b=G16),
                    magP[:, bass.ds(h.n, 1), :].rearrange("p a (b c) -> p (a b) c", c=1)
                    .to_broadcast([P, G16, G16]), ALU.mult).then_inc(wave1_done, 1)
                need(pool, wave1_done, h.n + 1)
                need(pool, b_mm, h.n - 1)
                need(pool, ghi_done, h.n - 1)
                need(pool, glo_done, h.n - 1)
                pool.tensor_tensor(
                    Grev[h.s2][:, :].rearrange("p (a b) -> p a b", b=G16),
                    wave1[:, :].rearrange("p (a b) -> p a b", b=G16),
                    magQ[:, bass.ds(h.n, 1), :].to_broadcast([P, G16, G16]),
                    ALU.mult).then_inc(grev_done, 1)

            def g_lo(h):
                need(pool, ghi_done, h.n + 1)
                need(pool, y_mm, (h.n - 3) * 2)
                pool.tensor_tensor(Glo[h.s4][:, :], Grev[h.s2][:, ::-1], Ghi[h.s4][:, :].bitcast(F32),
                                   ALU.subtract).then_inc(glo_done, 1)

            def m_matrix(h):
                need(pool, m1_done, h.n * 2 + 2)
                need(pool, b_mm, h.n - 1)
                pool.tensor_tensor(Mx[h.s2][:, 0:P], m1[h.s2][:, 0, :], m1[h.s2][:, 1, :],
                                   ALU.add).then_inc(mx_done, 1)

            def t_lo(h):
                need(pool, thi_done, h.n + 1)
                need(pool, y_mm, (h.n - 1) * 2)
                pool.tensor_tensor(Tlo[h.s2][:, :, :].rearrange("p a b -> p (a b)"), Traw[h.s2][:, ::-1],
                                   Thi[h.s2][:, :, :].rearrange("p a b -> p (a b)").bitcast(F32),
                                   ALU.subtract).then_inc(tlo_done, 1)

            def s_lo(h):
                need(pool, shi_done, h.n + 1)
                need(pool, y_mm, (h.n - 1) * 2)
                pool.tensor_tensor(Slo[h.s2][:, :], Sf[h.s2][:, :], Shi[h.s2][:, :].bitcast(F32),
                                   ALU.subtract).then_inc(slo_done, 1)

            def step(head):
                if head(0).there:
                    s_lo(head(0))
                if head(3).there:
                    g_table(head(3))
                    m_matrix(head(3))
                if head(1).there:
                    t_lo(head(1))
                if head(3).there:
                    g_lo(head(3))
                if head(4).there:
                    turn_parts(head(4))

            first = [Head(0, n, 0) for n in range(4)]
            turn_parts(first[0])
            turn_parts(first[1])
            pool.wait_ge(mag_done, 2)
            g_table(first[0])
            g_table(first[1])
            m_matrix(first[0])
            m_matrix(first[1])
            g_lo(first[0])
            g_lo(first[1])
            turn_parts(first[2])
            g_table(first[2])
            m_matrix(first[2])
            t_lo(first[0])
            g_lo(first[2])
            turn_parts(first[3])
            pool.wait_ge(mag_done, 4)
            run_steps(pool, step)

        @block.scalar
        def _(act):
            with nc.allow_non_contiguous_dma(reason="64 numbers"):
                act.dma_start(logs[:, N:N + 1], log_dt.rearrange("(h a) -> h a", a=1)).then_inc(in_logs, 16)
            with nc.allow_non_contiguous_dma(reason="expert rows of 16"):
                for e in range(E):
                    act.dma_start(B_nat[:, :, e * R:(e + 1) * R],
                                  Bw[e].rearrange("(j p) r -> p j r", p=P)).then_inc(in_B, 16)
            act.wait_ge(w_turned, 1)
            act.activation(Wt[:, 0:4, E:NW], psO[0][:, :].rearrange("p (c w) -> p c w", w=P),
                           ACT.Copy).then_inc(w_done, 1)
            act.activation(Wt[:, 4:8, E:NW], psO[1][:, :].rearrange("p (c w) -> p c w", w=P),
                           ACT.Copy).then_inc(w_done, 1)
            act.activation(Wt[:, :, 0:E], psZ[:, 0:NB * E].rearrange("p (c w) -> p c w", w=E),
                           ACT.Copy).then_inc(w_done, 1)

            def turns(h):
                need(act, frac1_done, h.n - 1)
                need(act, whole_done, h.n - 1)
                act.activation(turns_h[h.s2][:, :], egrid[:, :], ACT.Identity,
                               scale=col(tab1[:, VH, :], h), bias=quarter[:, :]).then_inc(turns_done, 1)
                act.activation(turns_t[h.s2][:, :], egrid[:, :], ACT.Identity,
                               scale=col(tab1[:, V, :], h), bias=quarter[:, :]).then_inc(turns_done, 1)

            def sines(h):
                need(act, frac_done, h.n + 1)
                need(act, wave1_done, h.n - 1)
                act.activation(wave[h.s2][:, :], fraction[h.s2][:, :], ACT.Sin, scale=TURN).then_inc(wave_done, 1)

            def g_hi(h):
                need(act, grev_done, h.n + 1)
                need(act, y_mm, (h.n - 3) * 2)
                act.activation(Ghi[h.s4][:, :], Grev[h.s2][:, ::-1], ACT.Copy).then_inc(ghi_done, 1)

            def m_parts(h):
                need(act, mx_done, h.n - 1)
                need(act, b_mm, h.n - 1)
                act.activation(m1[h.s2][:, 0, :], ident[:, :], ACT.Copy,
                               scale=col(tab2[:, AM, :], h)).then_inc(m1_done, 1)
                act.activation(m1[h.s2][:, 1, :], swap[:, :], ACT.Copy,
                               scale=col(tab2[:, BM, :], h)).then_inc(m1_done, 1)
                act.activation(Mx[h.s2][:, P:P + 1], col(tab2[:, CK, :], h), ACT.Copy).then_inc(kw_done, 1)

            def b_hi(h):
                need(act, b_mm, h.n + 1)
                need(act, k_out[h.s2], h.half * 16)
                act.activation(kcol[h.s2][:, 0:1], psB[:, 0, P:P + 1], ACT.Copy).then_inc(kcol_done, 1)
                act.activation(kcol[h.s2][:, 1:2], psB[:, 1, P:P + 1], ACT.Identity,
                               bias=Dcol[:, bass.ds(h.n, 1)]).then_inc(kcol_done, 1)
                need(act, s_mm, h.n - 1)
                act.activation(Bhi[h.s2][:, :, :], psB[:, :, 0:P], ACT.Copy).then_inc(bhi_done, 1)

            def t_hi(h):
                need(act, t_in[h.s2], h.half * 16 + 16)
                need(act, y_mm, (h.n - 1) * 2)
                act.activation(Thi[h.s2][:, :, :].rearrange("p a b -> p (a b)"), Traw[h.s2][:, ::-1],
                               ACT.Copy).then_inc(thi_done, 1)

            def x_hi(h, j):
                need(act, xt_done, h.n * 2 + j + 1)
                need(act, y_mm, (h.n - 1) * 2)
                act.activation(eo(Xhi[h.s2], j), psX[j][:, :], ACT.Copy).then_inc(xhi_done, 1)

            def first_state(h):
                need(act, s_mm, h.n + 1)
                need(act, shi_done, h.n - 1)
                need(act, slo_done, h.n - 1)
                act.activation(Sf[h.s2][:, 0:P], psS[:, 0:P], ACT.Copy).then_inc(s0_copied, 1)

            def s_hi(h):
                need(act, s_carried, h.n * 2 + 2)
                need(act, y_mm, (h.n - 1) * 2)
                act.activation(Shi[h.s2][:, :], Sf[h.s2][:, :], ACT.Copy).then_inc(shi_done, 1)

            def w_hi(h):
                need(act, wh_turned, h.n + 1)
                need(act, up_mm, (h.n - 1) * 2)
                act.activation(whi[h.s2][:, :], psWh, ACT.Copy).then_inc(whi_done, 1)

            def step(head):
                if head(0).there:
                    first_state(head(0))
                if head(4).there:
                    turns(head(4))
                if head(3).there:
                    m_parts(head(3))
                if head(1).there:
                    x_hi(head(1), 0)
                    x_hi(head(1), 1)
                if head(0).there:
                    s_hi(head(0))
                if head(2).there:
                    b_hi(head(2))
                if head(3).there:
                    sines(head(3))
                if head(1).there:
                    t_hi(head(1))
                if head(-1).there:
                    w_hi(head(-1))
                if head(3).there:
                    g_hi(head(3))

            first = [Head(0, n, 0) for n in range(4)]
            act.wait_ge(tabs_turned, 1)
            act.activation(tab1[:, :, :], psY[0][:, 0:4 * H].rearrange("p (t h) -> p t h", h=H),
                           ACT.Copy).then_inc(tab_done, 1)
            act.wait_ge(consts, 9)
            act.wait_ge(cols_set, 2)
            act.wait_ge(tab_done, 1)
            turns(first[0])
            turns(first[1])

            def magnitudes(part):
                act.wait_ge(rho_done, part + 1)
                heads = MAG_PARTS[part]
                act.activation(magP[:, heads, :], rho16[:, heads, :], ACT.Exp,
                               scale=float(G16)).then_inc(mag_done, 1)
                act.activation(magQ[:, heads, :], rho16[:, heads, :], ACT.Exp).then_inc(mag_done, 1)

            magnitudes(0)
            act.wait_ge(phases_done, 2)
            act.activation(sine[:, :, :], phase[:, :, :], ACT.Sin, scale=TURN).then_inc(sines_done, 1)
            act.activation(sine_half[:, :, :], phase[:, :, :], ACT.Sin, scale=TURN / 2).then_inc(sines_done, 1)
            sines(first[0])
            turns(first[2])
            x_hi(first[0], 0)
            x_hi(first[0], 1)
            sines(first[1])
            act.wait_ge(tabs_turned, 2)
            act.activation(tab2[:, :, :], psY[1][:, 0:5 * H].rearrange("p (t h) -> p t h", h=H),
                           ACT.Copy).then_inc(tab_done, 1)
            act.wait_ge(tab_done, 2)
            m_parts(first[0])
            m_parts(first[1])
            act.wait_ge(in_D, 16)
            b_hi(first[0])
            b_hi(first[1])
            g_hi(first[0])
            g_hi(first[1])
            turns(first[3])
            sines(first[2])
            m_parts(first[2])
            for j in range(2):
                act.wait_ge(b_turned, j + 1)
                act.activation(Bw_hi[:, j * 512:(j + 1) * 512], psO[1][:, :] if j else psZ[:, :],
                               ACT.Copy).then_inc(bhi_set, 1)
            t_hi(first[0])
            g_hi(first[2])
            magnitudes(1)
            run_steps(act, step)

        @block.vector
        def _(dve):
            count = [0]

            def link(ins):
                count[0] += 1
                ins.then_inc(v_set, 1)
                dve.wait_ge(v_set, count[0])

            def TS(o, a, s1, s2, op0, op1=None):
                link(dve.tensor_scalar(o, a, s1, s2, op0, op1) if op1 is not None
                     else dve.tensor_scalar(o, a, s1, None, op0))

            def TT(o, a, b, op):
                link(dve.tensor_tensor(o, a, b, op))

            def STT(o, a, s, b, op0, op1):
                link(dve.scalar_tensor_tensor(o, a, s, b, op0, op1))

            def exp(o, a, w):
                v, k, r, p, t = (ex[:, j, 0:w] for j in range(5))
                TS(v, a, 88.0, -87.0, ALU.min, ALU.max)
                TS(k, v, 1.4426950408889634, ROUND, ALU.mult, ALU.add)
                TS(k, k, ROUND, None, ALU.subtract)
                STT(r, k, -0.693359375, v, ALU.mult, ALU.add)
                STT(r, k, 2.12194440e-4, r, ALU.mult, ALU.add)
                TS(p, r, 1.0 / 5040, None, ALU.mult)
                for c in (1 / 720, 1 / 120, 1 / 24, 1 / 6, 0.5, 1.0):
                    STT(p, p, c, r, ALU.add, ALU.mult)
                TS(t.bitcast(I32), k, 127.0, None, ALU.add)
                TS(t.bitcast(I32), t.bitcast(I32), 23, None, ALU.logical_shift_left)
                STT(o, p, 1.0, t, ALU.add, ALU.mult)

            dve.memset(quarter[0:N, :], -0.25).then_inc(cols_set, 1)
            dve.memset(quarter[N:P, :], 0.0).then_inc(cols_set, 1)
            dve.wait_ge(in_logs, 32)
            exp(exps[:, :], logs[:, :], N + 1)
            dve.wait_ge(in_par, 32)
            ar, dt, Ai = exps[:, 0:N], exps[:, N:N + 1], A_im[:, :]
            rho = pack1[:, RHO, 0, :]
            dve.tensor_scalar(w[:, :], Ai, dt, None, ALU.mult).then_inc(w_set, 1)
            TS(rr[:, 0:N], ar, dt, -1.0, ALU.mult, ALU.mult)
            dve.wait_ge(w_set, 1)
            inv = 1.0 / (2.0 * np.pi)
            c1 = float(np.round(inv * 2**14) / 2**14)
            c2 = float(np.round((inv - c1) * 2**27) / 2**27)
            c3 = float(inv - c1 - c2)
            v, vh, vln = (pack1[:, t, 0, :] for t in (V, VH, VL))
            dve.tensor_scalar(v, w[:, :], inv, None, ALU.mult).then_inc(w_set, 1)
            link(dve.tensor_copy(w12[:, :], w[:, :]))
            w1 = w12[:, :].bitcast(F32)
            dve.tensor_tensor(w2[:, :], w[:, :], w1, ALU.subtract).then_inc(w_set, 1)
            TS(err[:, :], w1, c1, None, ALU.mult)
            dve.wait_ge(w_set, 3)
            link(dve.tensor_copy(v12[:, :], v))
            dve.tensor_copy(vh, v12[:, :].bitcast(F32)).then_inc(w_set, 1)
            dve.tensor_copy(rho, rr[:, 0:N]).then_inc(w_set, 1)
            TT(err[:, :], v12[:, :].bitcast(F32), err[:, :], ALU.subtract)
            for part, c in ((w1, c2), (w2[:, :], c1), (w2[:, :], c2), (w1, c3)):
                STT(err[:, :], part, -c, err[:, :], ALU.mult, ALU.add)
            link(dve.tensor_copy(vln, err[:, :]))
            dve.wait_ge(w_set, 5)
            dve.tensor_copy(pack1[:, :, 1, :], pack1[:, :, 0, :]).then_inc(pack1_done, 1)

            TS(rr[:, N:2 * N], rr[:, 0:N], float(Q), None, ALU.mult)
            exp(er[:, :], rr[:, :], 2 * N)
            e1, e256 = er[:, 0:N], er[:, N:2 * N]

            dve.wait_ge(consts, 9)
            dve.wait_ge(tab_done, 1)

            def exponents(heads, n):
                dve.tensor_tensor(rho16[:, heads, :],
                                  tab1[:, RHO, heads].rearrange("p (h a) -> p h a", a=1).to_broadcast([P, n, G16]),
                                  grid16[:, :].rearrange("p (a g) -> p a g", a=1).to_broadcast([P, n, G16]),
                                  ALU.mult).then_inc(rho_done, 1)

            exponents(MAG_PARTS[0], FIRST_HEADS)
            den = tmp[:, 0, :]
            dve.tensor_tensor(tmp[:, 1, :], Ai, Ai, ALU.mult).then_inc(w_set, 1)
            TT(den, ar, ar, ALU.mult)
            dve.wait_ge(w_set, 6)
            TT(den, den, tmp[:, 1, :], ALU.add)
            link(dve.reciprocal(den, den))

            def whole_turns(h):
                need(dve, turns_done, h.n * 2 + 2)
                need(dve, frac1_done, h.n - 1)
                dve.tensor_scalar(whole[h.s2][:, :], turns_t[h.s2][:, :], ROUND, ROUND,
                                  ALU.add, ALU.subtract).then_inc(whole_done, 1)

            def fractions(h):
                need(dve, frac1_done, h.n + 1)
                need(dve, frac_done, h.n)
                dve.scalar_tensor_tensor(frac2[:, :], egrid[:, :], col(tab1[:, VL, :], h), frac1[h.s2][:, :],
                                         ALU.mult, ALU.add).then_inc(frac2_done, 1)

            def clamp(h):
                need(dve, frac2_done, h.n + 1)
                need(dve, wave_done, h.n - 1)
                dve.tensor_scalar(fraction[h.s2][:, :], frac2[:, :], -0.5, 0.5,
                                  ALU.max, ALU.min).then_inc(frac_done, 1)

            first = [Head(0, n, 0) for n in range(4)]
            whole_turns(first[0])
            whole_turns(first[1])
            fractions(first[0])
            clamp(first[0])
            fractions(first[1])
            clamp(first[1])

            dve.wait_ge(sines_done, 2)
            STT(cm1[:, :, :], sine_half[:, :, :], -2.0, sine_half[:, :, :], ALU.mult, ALU.mult)
            nn, LL = pair[:, 0, :, :], pair[:, 1, :, :]
            dve.tensor_tensor(pack2[:, BR, 0, :], sine[:, 1, :], e256, ALU.mult).then_inc(w_set, 1)
            dve.tensor_tensor(nn[:, 1, :], e1, sine[:, 0, :], ALU.mult).then_inc(w_set, 1)
            dve.tensor_tensor(LL[:, 1, :], e1, sine[:, 0, :], ALU.mult).then_inc(w_set, 1)
            dve.scalar_tensor_tensor(pack2[:, LR, 0, :], cm1[:, 1, :], 1.0, e256,
                                     ALU.add, ALU.mult).then_inc(w_set, 1)
            TT(tmp[:, 1, :], e1, cm1[:, 0, :], ALU.mult)
            STT(nn[:, 0, :], e1, -1.0, tmp[:, 1, :], ALU.add, ALU.add)
            dve.wait_ge(w_set, 10)
            TS(LL[:, 0, :], nn[:, 0, :], 1.0, None, ALU.add)

            def times(o_re, o_im, a, b_re, b_im):
                dve.tensor_tensor(prod[:, 0, :, :], a, over(b_re), ALU.mult).then_inc(v_set, 1)
                dve.tensor_tensor(prod[:, 1, :, :], a, over(b_im), ALU.mult).then_inc(v_set, 1)
                count[0] += 2
                dve.wait_ge(v_set, count[0])
                dve.tensor_tensor(o_re, prod[:, 0, 0, :], prod[:, 1, 1, :], ALU.subtract).then_inc(v_set, 1)
                dve.tensor_tensor(o_im, prod[:, 0, 1, :], prod[:, 1, 0, :], ALU.add).then_inc(v_set, 1)
                count[0] += 2
                dve.wait_ge(v_set, count[0])

            def over(t):
                return t.rearrange("h (a n) -> h a n", a=1).to_broadcast([H, 2, N])

            times(CL[:, 0, :], CL[:, 1, :], C_nat[:, :, :].rearrange("h n c -> h c n"), nn[:, 0, :], nn[:, 1, :])
            times(QQ[:, 0, :], QQ[:, 1, :], CL[:, :, :], ar, Ai)
            STT(pack2[:, CK, :, :], QQ[:, :, :], -2.0, over(den), ALU.mult, ALU.mult)
            times(pack2[:, AM, 0, :], pack2[:, BM, 0, :], pack2[:, CK, :, :], LL[:, 0, :], LL[:, 1, :])
            dve.tensor_copy(pack2[:, 0:2, 1, :], pack2[:, 0:2, 0, :]).then_inc(pack2_done, 1)
            dve.tensor_scalar(pack2[:, 2:4, 1, :], pack2[:, 2:4, 0, :], -1.0, None,
                              ALU.mult).then_inc(pack2_done, 1)

            def x_lo(h, j):
                need(dve, xhi_done, h.n * 2 + j + 1)
                need(dve, y_mm, (h.n - 1) * 2)
                dve.tensor_tensor(eo(Xlo[h.s2], j), psX[j][:, :], eo(Xhi[h.s2], j).bitcast(F32),
                                  ALU.subtract).then_inc(xlo_done, 1)

            def largest(h):
                need(dve, z_mm, h.n + 1)
                need(dve, gate_done, h.n)
                dve.reduce_max(top[:, :], psZ[:, 0:E], axis=AX.X).then_inc(top_done, 1)

            def first_largest(h):
                need(dve, top_done, h.n + 1)
                dve.scalar_tensor_tensor(rank[:, :], psZ[:, 0:E], top[:, :], desc[:, :],
                                         ALU.is_equal, ALU.mult).then_inc(rank_done, 1)

            def first_best(h):
                need(dve, rank_done, h.n + 1)
                dve.reduce_max(best[:, :], rank[:, :], axis=AX.X).then_inc(best_done, 1)

            def gates(h):
                need(dve, best_done, h.n + 1)
                need(dve, wh_done, h.n)
                dve.tensor_scalar(gate[:, :], rank[:, :], best[:, :], top[:, :],
                                  ALU.is_equal, ALU.mult).then_inc(gate_done, 1)

            def gated(h):
                need(dve, gate_done, h.n + 1)
                need(dve, wh_turned, h.n)
                dve.tensor_tensor(wh[:, :].rearrange("p (e r) -> p e r", r=R),
                                  psZ[:, E:NW].rearrange("p (e r) -> p e r", r=R),
                                  gate[:, :].rearrange("p (e a) -> p e a", a=1)
                                  .to_broadcast([P, E, R]), ALU.mult).then_inc(wh_done, 1)

            def carry(h):
                need(dve, s0_copied, h.n + 1)
                for j in range(NS - 1):
                    need(dve, s_carried, h.n * 2 + j)
                    old, new = slice(j * P, (j + 1) * P), slice((j + 1) * P, (j + 2) * P)
                    for to, fr in ((slice(0, N), slice(N, P)), (slice(N, P), slice(0, N))):
                        dve.scalar_tensor_tensor(brought[to, :], Sf[h.s2][fr, old],
                                                 tab2[fr, BR, bass.ds(h.n, 1)], psS[to, new],
                                                 ALU.mult, ALU.add).then_inc(brought_done, 1)
                    need(dve, brought_done, h.n * 4 + j * 2 + 2)
                    dve.scalar_tensor_tensor(Sf[h.s2][:, new], Sf[h.s2][:, old], col(tab2[:, LR, :], h),
                                             brought[:, :], ALU.mult, ALU.add).then_inc(s_carried, 1)

            def b_lo(h):
                need(dve, bhi_done, h.n + 1)
                need(dve, s_mm, h.n - 1)
                dve.tensor_tensor(Blo[h.s2][:, :, :], psB[:, :, 0:P], Bhi[h.s2][:, :, :].bitcast(F32),
                                  ALU.subtract).then_inc(blo_done, 1)

            def w_lo(h):
                need(dve, whi_done, h.n + 1)
                need(dve, up_mm, (h.n - 1) * 2)
                dve.tensor_tensor(wlo[h.s2][:, :], psWh, whi[h.s2][:, :].bitcast(F32),
                                  ALU.subtract).then_inc(wlo_done, 1)

            def cut(h, j):
                need(dve, y_mm, h.n * 2 + j + 1)
                need(dve, z_mm, h.n)
                dve.tensor_tensor(Y[:, j, :, :].rearrange("p a b -> p (a b)"), psY[j][:, :],
                                  mask[:, j, :, :].rearrange("p a b -> p (a b)"),
                                  ALU.mult).then_inc(y_masked, 1)

            def add(h, j):
                need(dve, up_mm, h.n * 2 + j + 1)
                need(dve, x_in[h.s4], h.quarter * 16 + 16)
                need(dve, o_out[h.s2], h.half * 16)
                half = slice(j * 512, (j + 1) * 512)
                dve.tensor_tensor(ost[h.s2][:, half], psO[j][:, :], xt[h.s4][:, half],
                                  ALU.add).then_inc(added, 1)

            def step(head):
                if head(0).there:
                    carry(head(0))
                if head(-1).there:
                    largest(head(-1))
                if head(3).there:
                    fractions(head(3))
                if head(-1).there:
                    first_largest(head(-1))
                if head(3).there:
                    clamp(head(3))
                if head(-1).there:
                    first_best(head(-1))
                    gates(head(-1))
                if head(1).there:
                    x_lo(head(1), 0)
                if head(-1).there:
                    gated(head(-1))
                if head(1).there:
                    x_lo(head(1), 1)
                if head(2).there:
                    b_lo(head(2))
                if head(-1).there:
                    w_lo(head(-1))
                if head(4).there:
                    whole_turns(head(4))
                if head(0).there:
                    cut(head(0), 0)
                    cut(head(0), 1)
                if head(-1).there:
                    add(head(-1), 0)
                    add(head(-1), 1)

            x_lo(first[0], 0)
            x_lo(first[0], 1)
            exponents(MAG_PARTS[1], H - FIRST_HEADS)
            b_lo(first[0])
            b_lo(first[1])
            whole_turns(first[2])
            fractions(first[2])
            clamp(first[2])
            dve.wait_ge(in_len, 16)
            link(dve.tensor_copy(lens_f[:, :], lens_i[:, :]))
            for c in range(NB):
                dve.tensor_scalar(mask[:, c % 2, c // 2, :], lens_f[:, :], posn[:, c:c + 1], None,
                                  ALU.is_gt).then_inc(mask_done, 1)
            for j in range(2):
                dve.wait_ge(bhi_set, j + 1)
                dve.tensor_tensor(Bw_lo[:, j * 512:(j + 1) * 512], psO[1][:, :] if j else psZ[:, :],
                                  Bw_hi[:, j * 512:(j + 1) * 512].bitcast(F32),
                                  ALU.subtract).then_inc(blo_set, 1)
            dve.wait_ge(mask_done, NB)
            whole_turns(first[3])
            dve.wait_ge(tab_done, 2)
            run_steps(dve, step)

        @block.tensor
        def _(pe):
            pe.wait_ge(consts, 9)
            pe.wait_ge(in_A, 16)
            pe.wait_ge(in_rw, 16)
            for c in range(NB):
                cols = slice((c % 4) * P, (c % 4 + 1) * P)
                pe.transpose(psO[c // 4][:, cols], A_nat[:, c * P:(c + 1) * P], ident[:, :])
            for c in range(NB):
                last = pe.transpose(psZ[:, c * E:(c + 1) * E], route_nat[:, c * P:(c + 1) * P],
                                    ident[0:E, 0:E])
            last.then_inc(w_turned, 1)
            def three(dst, pairs, first, last):
                n = 3 * len(pairs)
                i = 0
                for (ah, al), (bh, bl) in pairs:
                    for a, b in ((ah, bh), (ah, bl), (al, bh)):
                        mm = pe.matmul(dst, a, b, start=first and i == 0, stop=last and i == n - 1,
                                       skip_group_check=True)
                        i += 1
                return mm

            def turn_x(h, j):
                need(pe, x_in[h.s4], h.quarter * 16 + 16)
                need(pe, xhi_done, h.n * 2 - 1 + j)
                need(pe, xlo_done, h.n * 2 - 1 + j)
                for c in range(NE):
                    at = (2 * c + j) * P
                    last = pe.transpose(psX[j][:, c * P:(c + 1) * P], xt[h.s4][:, at:at + P], ident[:, :])
                last.then_inc(xt_done, 1)

            def project(h, j):
                need(pe, y_masked, h.n * 2 + j + 1)
                if isinstance(h.n, int) and h.n == 0:
                    pe.wait_ge(blo_set, 2)
                if j == 0:
                    need(pe, wlo_done, h.n)
                for c in range(NE):
                    last = pe.matmul(psZ[:, 0:NW], Y[:, j, c, :], Wt[:, 2 * c + j, :],
                                     start=(j == 0 and c == 0), stop=(j == 1 and c == NE - 1),
                                     skip_group_check=True)
                if j == 1:
                    last.then_inc(z_mm, 1)

            def bring(h):
                need(pe, xhi_done, h.n * 2 + 2)
                need(pe, xlo_done, h.n * 2 + 2)
                need(pe, bhi_done, h.n + 1)
                need(pe, blo_done, h.n + 1)
                need(pe, s_carried, h.n * 2)
                w = NS * P
                three(psS[:, 0:w],
                      [((Bhi[h.s2][:, j, :], Blo[h.s2][:, j, :]), (Xhi[h.s2][:, j, 0:w], Xlo[h.s2][:, j, 0:w]))
                       for j in range(2)], True, True).then_inc(s_mm, 1)

            def inputs(h):
                need(pe, added, (h.n - 3) * 2 - 1)
                need(pe, blo_done, h.n)
                need(pe, mx_done, h.n + 1)
                need(pe, kw_done, h.n + 1)
                need(pe, grev_done, h.n + 1)
                for j in range(2):
                    last = pe.matmul(psB[:, j, :], Grev[h.s2][:, j * P:(j + 1) * P],
                                     Mx[h.s2][:, :], start=True, stop=True, skip_group_check=True)
                last.then_inc(b_mm, 1)

            def within(h, j):
                need(pe, thi_done, h.n + 1)
                need(pe, tlo_done, h.n + 1)
                T = [(Thi[h.s2][:, j, :], Tlo[h.s2][:, j, :]) for j in range(2)]
                X = [(Xhi[h.s2][:, j, :], Xlo[h.s2][:, j, :]) for j in range(2)]
                need(pe, y_masked, h.n * 2 - 1 + j)
                three(psY[j][:, :], [(T[0], X[j])] + [(T[1], X[0])] * j, True, False)

            def from_states(h):
                need(pe, shi_done, h.n + 1)
                need(pe, slo_done, h.n + 1)
                need(pe, glo_done, h.n + 1)
                for j in range(2):
                    G = tuple(g[h.s4][:, j * P:(j + 1) * P] for g in (Ghi, Glo))
                    three(psY[j][:, P:512], [(G, (Shi[h.s2][:, :], Slo[h.s2][:, :]))],
                          False, True).then_inc(y_mm, 1)

            def turn_wh(h):
                need(pe, wh_done, h.n + 1)
                need(pe, wlo_done, h.n)
                pe.transpose(psWh, wh[:, :], ident[:, :]).then_inc(wh_turned, 1)

            def up(h, ahead):
                need(pe, whi_done, h.n + 1)
                need(pe, wlo_done, h.n + 1)
                if ahead.there:
                    need(pe, blo_done, ahead.n + 1)
                for j in range(2):
                    need(pe, added, h.n * 2 - 1 + j)
                    half = slice(j * 512, (j + 1) * 512)
                    three(psO[j][:, :], [((whi[h.s2][:, :], wlo[h.s2][:, :]),
                                          (Bw_hi[:, half], Bw_lo[:, half]))],
                          True, True).then_inc(up_mm, 1)

            def step(head):
                if head(0).there:
                    bring(head(0))
                if head(-1).there:
                    project(head(-1), 0)
                if head(-1).there:
                    project(head(-1), 1)
                if head(1).there:
                    turn_x(head(1), 0)
                    turn_x(head(1), 1)
                if head(2).there:
                    inputs(head(2))
                if head(0).there:
                    within(head(0), 0)
                    within(head(0), 1)
                if head(-1).there:
                    turn_wh(head(-1))
                if head(0).there:
                    from_states(head(0))
                if head(-1).there:
                    up(head(-1), head(2))

            def turn_tables(pack, bank_, n):
                for t in range(n):
                    last = pe.transpose(bank_[:, t * H:(t + 1) * H],
                                        pack[:, t, :, :].rearrange("h a n -> h (a n)"), ident[0:H, 0:H])
                last.then_inc(tabs_turned, 1)

            first = [Head(0, n, 0) for n in range(2)]
            pe.wait_ge(pack1_done, 1)
            turn_tables(pack1, psY[0], 4)
            turn_x(first[0], 0)
            turn_x(first[0], 1)
            pe.wait_ge(pack2_done, 2)
            turn_tables(pack2, psY[1], 5)
            pe.wait_ge(w_done, 3)
            inputs(first[0])
            inputs(first[1])
            pe.wait_ge(in_B, 16 * E)
            for c in range(NB):
                cols = slice((c % 4) * P, (c % 4 + 1) * P)
                last = pe.transpose((psO[1] if c // 4 else psZ)[:, cols], B_nat[:, c, :], ident[:, :])
                if c % 4 == 3:
                    last.then_inc(b_turned, 1)
            pe.wait_ge(tab_done, 2)
            run_steps(pe, step)


_INS = ['x', 'itok_B_8_3872', 'L0_cond_log_dt', 'L0_cond_C', 'L0_cond_log_A_real', 'L0_cond_A_imag',
        'L0_cond_D', 'L0_ffn_route_w', 'L0_ffn_A', 'L0_ffn_Bw']


def kernel(**inputs):
    import numpy as _np
    import concourse.bacc as _bacc
    from concourse import mybir as _mybir
    from concourse.bass_utils import run_bass_kernel_spmd as _run

    nc = _bacc.Bacc("TRN2", target_bir_lowering=False, num_devices=1)
    arrays, args = {}, []
    for name in _INS:
        a = _np.ascontiguousarray(inputs[name])
        arrays[f"in_{name}_dram"] = a
        args.append(nc.dram_tensor(f"in_{name}_dram", a.shape, _mybir.dt.from_np(a.dtype), kind="ExternalInput").ap())
    shape = inputs['x'].shape
    args.append(nc.dram_tensor("out_0_dram", shape, _mybir.dt.float32, kind="ExternalOutput").ap())
    conv_ffn_kernel(nc, *args)
    r = _run(nc, [arrays], core_ids=[0])
    return r.results[0]["out_0_dram"]
```

```python
import concourse.bass as bass
import numpy as np
from concourse import mybir
from contextlib import ExitStack


F32 = mybir.dt.float32
F32R = mybir.dt.float32r
I32 = mybir.dt.int32
ALU = mybir.AluOpType
ACT = mybir.ActivationFunctionType
AX = mybir.AxisListType

P = 128
ROUND = 12582912.0
TURN = 6.283185


def conv_ffn_kernel(nc, x, lens, log_dt, Cw, log_A_real, A_imag, D, route_w, Aw, Bw, out):
    B, H, L = x.shape
    N = A_imag.shape[1]
    E, R, _ = Aw.shape
    ER = E * R
    NB = L // P
    NE = NB // 2
    Q = 2 * P
    NS = NE - 1
    NW = ER + E
    HALF = L // 2
    G16 = 16
    assert B == P and 2 * N == P and ER == P and HALF == 512 and H % 8 == 0

    ctx = ExitStack()
    with ctx:
        def sb(name, shape, dt=F32):
            return ctx.enter_context(nc.sbuf_tensor(name, shape, dt))

        def bank(name):
            return ctx.enter_context(nc.psum_tensor(name, [P, 512], F32))

        def sem(name):
            return ctx.enter_context(nc.semaphore(name))

        ident = sb("ident", [P, P])
        twin = sb("twin", [P, P])
        egrid = sb("egrid", [P, Q])
        grid16 = sb("grid16", [P, G16])
        desc = sb("desc", [P, E])
        quarter = sb("quarter", [P, 1])
        posn = sb("posn", [P, NB])
        lens_i = sb("lens_i", [P, P], I32)
        lens_f = sb("lens_f", [P, P])
        mask = sb("mask", [P, 2, NE, P])
        zeros = sb("zeros", [1, P])
        Dcol = sb("Dcol", [P, H])
        route_nat = sb("route_nat", [E, L])
        A_nat = sb("A_nat", [P, L])
        B_nat = sb("B_nat", [P, NB, ER])
        Wt = sb("Wt", [P, NB, NW])
        Bw_hi = sb("Bw_hi", [P, L], F32R)
        Bw_lo = sb("Bw_lo", [P, L], F32R)
        logs = sb("logs", [H, N + 1])
        A_im = sb("A_im", [H, N])
        C_nat = sb("C_nat", [H, N, 2])
        V, VH, VL, RHO = range(4)
        LR, M0, M1, BR, CK = range(5)
        pack1 = sb("pack1", [H, 4, 2, N])
        pack2 = sb("pack2", [H, 5, 2, N])
        tab1 = sb("tab1", [P, 4, H])
        tab2 = sb("tab2", [P, 5, H])
        RHO_PARTS = [(0, H // 8), (H // 8, 3 * H // 8), (H // 2, H // 2)]
        rho16 = sb("rho16", [P, H, G16])
        magP = sb("magP", [P, H, G16])
        magQ = sb("magQ", [P, H, G16])
        ex = sb("ex", [H, 5, 2 * N])
        exps = sb("exps", [H, N + 1])
        w = sb("w", [H, N])
        w12 = sb("w12", [H, N], F32R)
        w2 = sb("w2", [H, N])
        v12 = sb("v12", [H, N], F32R)
        em1 = sb("em1", [H, N])
        sq = sb("sq", [H, 2, N])
        den = sb("den", [H, N])
        rden = sb("rden", [H, N])
        err = sb("err", [H, N])
        turns_of = sb("turns_of", [H, 2, N])
        Lm1 = sb("Lm1", [H, 2, N])
        Lre = sb("Lre", [H, N])
        prod = sb("prod", [H, 2, 2, N])
        cprod = sb("cprod", [H, 2, 2, N])
        Craw = sb("Craw", [H, 2, N])
        CA = sb("CA", [H, 2, N])
        warm = sb("warm", [P, 1])
        phase = sb("phase", [H, 2, N])
        rr = sb("rr", [H, 2 * N])
        er = sb("er", [H, 2 * N])
        sine = sb("sine", [H, 2, N])
        sine_half = sb("sine_half", [H, 2, N])
        cm1 = sb("cm1", [H, 2, N])
        xt = [sb(f"xt{s}", [P, L]) for s in range(4)]
        Xhi = [sb(f"Xhi{s}", [P, 2, HALF], F32R) for s in range(2)]
        Xlo = [sb(f"Xlo{s}", [P, 2, HALF], F32R) for s in range(2)]
        xeven = sb("xeven", [P, HALF])
        turns_h = [sb(f"turns_h{s}", [P, Q]) for s in range(2)]
        turns_t = [sb(f"turns_t{s}", [P, Q]) for s in range(2)]
        whole = [sb(f"whole{s}", [P, Q]) for s in range(2)]
        frac1 = [sb(f"frac1_{s}", [P, Q]) for s in range(2)]
        frac2 = sb("frac2", [P, Q])
        fraction = [sb(f"fraction{s}", [P, Q]) for s in range(2)]
        wave = [sb(f"wave_{s}", [P, Q]) for s in range(2)]
        wave1 = sb("wave1", [P, Q])
        Grev = [sb(f"Grev{s}", [P, Q]) for s in range(2)]
        Ghi = [sb(f"Ghi{s}", [P, Q], F32R) for s in range(4)]
        Glo = [sb(f"Glo{s}", [P, Q], F32R) for s in range(4)]
        Mx = [sb(f"Mx{s}", [P, P + 1]) for s in range(2)]
        kcol = [sb(f"kcol{s}", [P, 2]) for s in range(2)]
        Bhi = [sb(f"Bhi{s}", [P, 2, P], F32R) for s in range(2)]
        Blo = [sb(f"Blo{s}", [P, 2, P], F32R) for s in range(2)]
        Traw = [sb(f"Traw{s}", [P, Q]) for s in range(2)]
        Thi = [sb(f"Thi{s}", [P, 2, P], F32R) for s in range(2)]
        Tlo = [sb(f"Tlo{s}", [P, 2, P], F32R) for s in range(2)]
        Sf = [sb(f"Sf{s}", [P, NS * P]) for s in range(2)]
        brought = sb("brought", [P, P])
        Shi = [sb(f"Shi{s}", [P, NS * P], F32R) for s in range(2)]
        Slo = [sb(f"Slo{s}", [P, NS * P], F32R) for s in range(2)]
        Y = sb("Y", [P, 2, NE, P])
        top = sb("top", [P, 1])
        rank = sb("rank", [P, E])
        best = sb("best", [P, 1])
        gate = sb("gate", [P, E])
        wh = sb("wh", [P, ER])
        whi = [sb(f"whi{s}", [P, P], F32R) for s in range(2)]
        wlo = [sb(f"wlo{s}", [P, P], F32R) for s in range(2)]
        ost = [sb(f"ost{s}", [P, L]) for s in range(2)]

        kdram = nc.dram_tensor("kdram", [2, P + Q], F32, kind="Internal").ap()

        psX = [bank("psXe"), bank("psXo")]
        psY = [bank("psYe"), bank("psYo")]
        psS = bank("psS")
        psZ = bank("psZ")
        psO = [bank("psO0"), bank("psO1")]
        psB = psO[0][:, :].rearrange("p (j w) -> p j w", j=2)[:, :, 0:P + 1]
        psWh = psZ[:, 256:256 + P]

        in_logs = sem("in_logs")
        in_par = sem("in_par")
        in_len = sem("in_len")
        in_D = sem("in_D")
        in_rw = sem("in_rw")
        in_A = sem("in_A")
        in_B = sem("in_B")
        pad_done = sem("pad_done")
        consts = sem("consts")
        cols_set = sem("cols_set")
        zero_row = sem("zero_row")
        v_set = sem("v_set")
        phases_done = sem("phases_done")
        sines_done = sem("sines_done")
        pack1_done = sem("pack1_done")
        pack2_done = sem("pack2_done")
        exps_set = sem("exps_set")
        den_set = sem("den_set")
        rden_set = sem("rden_set")
        ca_set = sem("ca_set")
        g_set = sem("g_set")
        tabs_turned = sem("tabs_turned")
        tab_done = sem("tab_done")
        rho_done = sem("rho_done")
        mag_done = sem("mag_done")
        mask_done = sem("mask_done")
        w_turned = sem("w_turned")
        w_done = sem("w_done")
        b_turned = sem("b_turned")
        bhi_set = sem("bhi_set")
        blo_set = sem("blo_set")
        x_in = [sem(f"x_in{s}") for s in range(4)]
        k_out = [sem(f"k_out{s}") for s in range(2)]
        t_in = [sem(f"t_in{s}") for s in range(2)]
        o_out = [sem(f"o_out{s}") for s in range(2)]
        turns_done = sem("turns_done")
        whole_done = sem("whole_done")
        frac1_done = sem("frac1_done")
        frac2_done = sem("frac2_done")
        frac_done = sem("frac_done")
        wave_done = sem("wave_done")
        wave1_done = sem("wave1_done")
        grev_done = sem("grev_done")
        ghi_done = sem("ghi_done")
        glo_done = sem("glo_done")
        mx_done = sem("mx_done")
        b_mm = sem("b_mm")
        kcol_done = sem("kcol_done")
        bhi_done = sem("bhi_done")
        blo_done = sem("blo_done")
        thi_done = sem("thi_done")
        tlo_done = sem("tlo_done")
        xt_done = sem("xt_done")
        xhi_done = sem("xhi_done")
        xeven_done = sem("xeven_done")
        xlo_even = sem("xlo_even")
        xlo_odd = sem("xlo_odd")
        s_mm = sem("s_mm")
        s0_copied = sem("s0_copied")
        brought_done = sem("brought_done")
        s_carried = sem("s_carried")
        shi_done = sem("shi_done")
        slo_done = sem("slo_done")
        y_mm = sem("y_mm")
        y_masked = sem("y_masked")
        z_mm = sem("z_mm")
        top_done = sem("top_done")
        rank_done = sem("rank_done")
        best_done = sem("best_done")
        gate_done = sem("gate_done")
        wh_done = sem("wh_done")
        wh_turned = sem("wh_turned")
        whi_done = sem("whi_done")
        wlo_done = sem("wlo_done")
        up_mm = sem("up_mm")
        added = sem("added")

        block = ctx.enter_context(nc.Block())

        TURN_STEPS = 8

        class Head:
            def __init__(self, q, k, d):
                self.n = q * TURN_STEPS + (k + d)
                self.half = q * (TURN_STEPS // 2) + (k + d) // 2
                self.quarter = q * (TURN_STEPS // 4) + (k + d) // 4
                self.s2 = (k + d) % 2
                self.s4 = (k + d) % 4
                self.there = not isinstance(q, int) or 0 <= self.n < H

        def is_head(h, *numbers):
            return isinstance(h.n, int) and h.n in numbers

        def exponents(eng, start, n):
            heads = slice(start, start + n)
            eng.tensor_tensor(rho16[:, heads, :],
                              tab1[:, RHO, heads].rearrange("p (h a) -> p h a", a=1).to_broadcast([P, n, G16]),
                              grid16[:, :].rearrange("p (a g) -> p a g", a=1).to_broadcast([P, n, G16]),
                              ALU.mult).then_inc(rho_done, 1)

        def need(eng, s, count):
            if not isinstance(count, int) or count > 0:
                eng.wait_ge(s, count)

        def run_steps(eng, step):
            for i in range(4):
                step(lambda d, i=i: Head(0, i, d))
            with eng.Fori(0, (H - 8) // TURN_STEPS) as q:
                for k in range(4, 4 + TURN_STEPS):
                    step(lambda d, k=k: Head(q, k, d))
            for i in range(H - 4, H + 1):
                step(lambda d, i=i: Head(0, i, d))

        def col(t, h):
            return t[:, bass.ds(h.n, 1)]

        def eo(t, j):
            return t[:, j, :]

        @block.sync
        def _(sp):
            sp.dma_start(logs[:, 0:N], log_A_real).then_inc(in_logs, 16)
            sp.dma_start(A_im[:, :], A_imag).then_inc(in_par, 16)
            sp.dma_start(C_nat[:, :, :], Cw).then_inc(in_par, 16)

            def head_rows(t, h):
                return bass.AP(t.tensor, h.n * L, [[H * L, P], [1, L]])

            def load_x(h):
                need(sp, added, (h.n - 3) * 2)
                sp.dma_start(xt[h.s4][:, :], head_rows(x, h)).then_inc(x_in[h.s4], 16)

            def turn_kernel(h):
                need(sp, thi_done, h.n - 1)
                need(sp, tlo_done, h.n - 1)
                need(sp, kcol_done, h.n * 2 + 2)
                with nc.allow_non_contiguous_dma(reason="a column of numbers"):
                    sp.dma_start(bass.AP(kdram.tensor, h.s2 * (P + Q), [[1, P], [P, 2], [1, 1]]),
                                 kcol[h.s2][:, :].rearrange("p (j a) -> p j a", a=1)).then_inc(k_out[h.s2], 16)
                need(sp, k_out[h.s2], h.half * 16 + 16)
                sp.dma_start(Traw[h.s2][:, :],
                             bass.AP(kdram.tensor, h.s2 * (P + Q), [[1, P], [1, Q]])
                             ).then_inc(t_in[h.s2], 16)

            def store_half(h, j):
                need(sp, added, h.n * 2 + j + 1)
                half = slice(j * 512, (j + 1) * 512)
                sp.dma_start(bass.AP(out.tensor, h.n * L + j * 512, [[H * L, P], [1, 512]]),
                             ost[h.s2][:, half]).then_inc(o_out[h.s2], 16)

            def store(h):
                need(sp, added, h.n * 2 + 2)
                sp.dma_start(head_rows(out, h), ost[h.s2][:, :]).then_inc(o_out[h.s2], 16)

            def step(head):
                if head(2).there:
                    load_x(head(2))
                    turn_kernel(head(2))
                if head(-1).there and not is_head(head(-1), H - 1):
                    store(head(-1))

            load_x(Head(0, 0, 0))
            sp.dma_start(A_nat[:, :], Aw.rearrange("e r d -> (e r) d")).then_inc(in_A, 16)
            sp.dma_start(route_nat[:, :], route_w).then_inc(in_rw, 16)
            sp.wait_ge(zero_row, 2)
            sp.dma_start(Dcol[P - 1:P, :], D.rearrange("(a h) -> a h", a=1)).then_inc(in_D, 16)
            for s in range(2):
                sp.dma_start(kdram[s:s + 1, Q:Q + P], zeros[:, :]).then_inc(pad_done, 16)
            with nc.allow_non_contiguous_dma(reason="expert rows of 16"):
                for e in range(E):
                    sp.dma_start(B_nat[:, :, e * R:(e + 1) * R],
                                 Bw[e].rearrange("(j p) r -> p j r", p=P)).then_inc(in_B, 16)
            sp.dma_start(lens_i[:, :], lens.partition_broadcast(P)).then_inc(in_len, 16)
            load_x(Head(0, 1, 0))
            sp.wait_ge(pad_done, 32)
            for n in range(2):
                turn_kernel(Head(0, n, 0))
            run_steps(sp, step)
            for j in range(2):
                store_half(Head(0, H - 1, 0), j)
            for s in range(2):
                sp.wait_ge(o_out[s], 16 * (H // 2 + s))
                sp.wait_ge(k_out[s], 16 * (H // 2))
                sp.wait_ge(t_in[s], 16 * (H // 2))

        @block.gpsimd
        def _(pool):
            pool.memset(zeros[:, :], 0.0).then_inc(zero_row, 1)
            pool.memset(Dcol[:, :], 0.0).then_inc(zero_row, 1)
            pool.memset(ident[:, :], 0.0).then_inc(consts, 1)
            pool.memset(twin[:, :], 0.0).then_inc(consts, 1)
            pool.iota(egrid[:, :], pattern=[[-1, Q]], base=Q - 1, channel_multiplier=0,
                      allow_small_or_imprecise_dtypes=True).then_inc(consts, 1)
            pool.iota(grid16[:, :], pattern=[[-1, G16]], base=G16 - 1, channel_multiplier=0,
                      allow_small_or_imprecise_dtypes=True).then_inc(consts, 1)
            pool.iota(desc[:, :], pattern=[[-1, E]], base=E, channel_multiplier=0,
                      allow_small_or_imprecise_dtypes=True).then_inc(consts, 1)
            pool.iota(posn[:, :], pattern=[[P, NB]], base=0, channel_multiplier=1,
                      allow_small_or_imprecise_dtypes=True).then_inc(consts, 1)
            pool.wait_ge(consts, 6)
            pool.affine_select(out=ident[:, :], in_=ident[:, :], compare_op=ALU.not_equal, fill=1.0,
                               base=0, pattern=[[-1, P]], channel_multiplier=1).then_inc(consts, 1)
            pool.affine_select(out=twin[:, :], in_=twin[:, :], compare_op=ALU.not_equal, fill=1.0,
                               base=N, pattern=[[-1, P]], channel_multiplier=1).then_inc(consts, 1)
            pool.wait_ge(consts, 8)
            pool.affine_select(out=twin[:, :], in_=twin[:, :], compare_op=ALU.not_equal, fill=1.0,
                               base=-N, pattern=[[-1, P]], channel_multiplier=1).then_inc(consts, 1)
            pool.wait_ge(consts, 9)
            pool.affine_select(out=twin[:, :], in_=twin[:, :], compare_op=ALU.not_equal, fill=1.0,
                               base=0, pattern=[[-1, P]], channel_multiplier=1).then_inc(consts, 1)

            ar, Ai = exps[:, 0:N], A_im[:, :]
            C_parts = C_nat[:, :, :].rearrange("h n c -> h c n")

            def over(t):
                return t.rearrange("h (a n) -> h a n", a=1).to_broadcast([H, 2, N])

            pool.wait_ge(in_par, 32)
            pool.tensor_tensor(sq[:, 1, :], Ai, Ai, ALU.mult).then_inc(g_set, 1)
            pool.tensor_tensor(cprod[:, 1, :, :], C_parts, over(Ai), ALU.mult).then_inc(g_set, 1)
            pool.wait_ge(exps_set, 1)
            pool.tensor_tensor(sq[:, 0, :], ar, ar, ALU.mult).then_inc(g_set, 1)
            pool.wait_ge(g_set, 3)
            pool.tensor_tensor(den[:, :], sq[:, 0, :], sq[:, 1, :], ALU.add).then_inc(den_set, 1)
            pool.tensor_tensor(cprod[:, 0, :, :], C_parts, over(ar), ALU.mult).then_inc(g_set, 1)
            pool.wait_ge(g_set, 4)
            pool.tensor_tensor(Craw[:, 0, :], cprod[:, 0, 0, :], cprod[:, 1, 1, :], ALU.subtract).then_inc(g_set, 1)
            pool.tensor_tensor(Craw[:, 1, :], cprod[:, 0, 1, :], cprod[:, 1, 0, :], ALU.add).then_inc(g_set, 1)
            pool.wait_ge(g_set, 6)
            pool.wait_ge(tab_done, 1)
            exponents(pool, *RHO_PARTS[1])
            pool.wait_ge(rden_set, 2)
            pool.tensor_tensor(CA[:, :, :], Craw[:, :, :], over(rden[:, :]), ALU.mult).then_inc(ca_set, 1)
            exponents(pool, *RHO_PARTS[2])

            def turn_parts(h):
                need(pool, whole_done, h.n + 1)
                need(pool, frac2_done, h.n - 1)
                pool.tensor_tensor(frac1[h.s2][:, :], whole[h.s2][:, :], turns_h[h.s2][:, :],
                                   ALU.subtract).then_inc(frac1_done, 1)

            def g_table(h):
                need(pool, wave_done, h.n + 1)
                need(pool, grev_done, h.n)
                pool.tensor_tensor(
                    wave1[:, :].rearrange("p (a b) -> p a b", b=G16),
                    wave[h.s2][:, :].rearrange("p (a b) -> p a b", b=G16),
                    magP[:, bass.ds(h.n, 1), :].rearrange("p a (b c) -> p (a b) c", c=1)
                    .to_broadcast([P, G16, G16]), ALU.mult).then_inc(wave1_done, 1)
                need(pool, wave1_done, h.n + 1)
                need(pool, b_mm, h.n - 1)
                need(pool, ghi_done, h.n - 1)
                need(pool, glo_done, h.n - 1)
                pool.tensor_tensor(
                    Grev[h.s2][:, :].rearrange("p (a b) -> p a b", b=G16),
                    wave1[:, :].rearrange("p (a b) -> p a b", b=G16),
                    magQ[:, bass.ds(h.n, 1), :].to_broadcast([P, G16, G16]),
                    ALU.mult).then_inc(grev_done, 1)

            def g_lo(h):
                need(pool, ghi_done, h.n + 1)
                need(pool, y_mm, (h.n - 3) * 2)
                pool.tensor_tensor(Glo[h.s4][:, :], Grev[h.s2][:, ::-1], Ghi[h.s4][:, :].bitcast(F32),
                                   ALU.subtract).then_inc(glo_done, 1)

            def t_lo(h):
                need(pool, thi_done, h.n + 1)
                need(pool, y_mm, (h.n - 1) * 2)
                pool.tensor_tensor(Tlo[h.s2][:, :, :].rearrange("p a b -> p (a b)"), Traw[h.s2][:, ::-1],
                                   Thi[h.s2][:, :, :].rearrange("p a b -> p (a b)").bitcast(F32),
                                   ALU.subtract).then_inc(tlo_done, 1)

            def x_lo(h):
                need(pool, xeven_done, h.n + 1)
                need(pool, y_mm, (h.n - 1) * 2)
                pool.tensor_tensor(Xlo[h.s2][:, 0, :], xeven[:, :], Xhi[h.s2][:, 0, :].bitcast(F32),
                                   ALU.subtract).then_inc(xlo_even, 1)

            def s_lo(h):
                need(pool, shi_done, h.n + 1)
                need(pool, y_mm, (h.n - 1) * 2)
                pool.tensor_tensor(Slo[h.s2][:, :], Sf[h.s2][:, :], Shi[h.s2][:, :].bitcast(F32),
                                   ALU.subtract).then_inc(slo_done, 1)

            def step(head):
                if head(0).there and not is_head(head(0), 0):
                    s_lo(head(0))
                if head(1).there:
                    x_lo(head(1))
                if head(3).there:
                    g_table(head(3))
                if head(1).there:
                    t_lo(head(1))
                if head(3).there:
                    g_lo(head(3))
                if head(4).there:
                    turn_parts(head(4))

            first = [Head(0, n, 0) for n in range(4)]
            turn_parts(first[0])
            x_lo(first[0])
            pool.wait_ge(mag_done, 2)
            g_table(first[0])
            turn_parts(first[1])
            g_table(first[1])
            g_lo(first[0])
            turn_parts(first[2])
            g_lo(first[1])
            t_lo(first[0])
            g_table(first[2])
            s_lo(first[0])
            turn_parts(first[3])
            g_lo(first[2])
            run_steps(pool, step)

        @block.scalar
        def _(act):
            with nc.allow_non_contiguous_dma(reason="64 numbers"):
                act.dma_start(logs[:, N:N + 1], log_dt.rearrange("(h a) -> h a", a=1)).then_inc(in_logs, 16)
            act.wait_ge(cols_set, 2)
            act.activation(warm[:, :], quarter[:, :], ACT.Sin)

            def turns(h):
                need(act, frac1_done, h.n - 1)
                need(act, whole_done, h.n - 1)
                act.activation(turns_h[h.s2][:, :], egrid[:, :], ACT.Identity,
                               scale=col(tab1[:, VH, :], h), bias=quarter[:, :]).then_inc(turns_done, 1)
                act.activation(turns_t[h.s2][:, :], egrid[:, :], ACT.Identity,
                               scale=col(tab1[:, V, :], h), bias=quarter[:, :]).then_inc(turns_done, 1)

            def sines(h):
                need(act, frac_done, h.n + 1)
                need(act, wave1_done, h.n - 1)
                act.activation(wave[h.s2][:, :], fraction[h.s2][:, :], ACT.Sin, scale=TURN).then_inc(wave_done, 1)

            def g_hi(h):
                need(act, grev_done, h.n + 1)
                need(act, y_mm, (h.n - 3) * 2)
                act.activation(Ghi[h.s4][:, :], Grev[h.s2][:, ::-1], ACT.Copy).then_inc(ghi_done, 1)

            def m_matrix(h):
                need(act, b_mm, h.n - 1)
                for j, table in enumerate((M0, M1)):
                    act.activation(Mx[h.s2][:, j * N:(j + 1) * N], twin[:, j * N:(j + 1) * N], ACT.Copy,
                                   scale=col(tab2[:, table, :], h)).then_inc(mx_done, 1)
                act.activation(Mx[h.s2][:, P:P + 1], col(tab2[:, CK, :], h), ACT.Copy).then_inc(mx_done, 1)

            def b_hi(h):
                need(act, b_mm, h.n + 1)
                need(act, k_out[h.s2], h.half * 16)
                act.activation(kcol[h.s2][:, 0:1], psB[:, 0, P:P + 1], ACT.Copy).then_inc(kcol_done, 1)
                act.activation(kcol[h.s2][:, 1:2], psB[:, 1, P:P + 1], ACT.Identity,
                               bias=Dcol[:, bass.ds(h.n, 1)]).then_inc(kcol_done, 1)
                need(act, s_mm, h.n - 1)
                act.activation(Bhi[h.s2][:, :, :], psB[:, :, 0:P], ACT.Copy).then_inc(bhi_done, 1)

            def t_hi(h):
                need(act, t_in[h.s2], h.half * 16 + 16)
                need(act, y_mm, (h.n - 1) * 2)
                act.activation(Thi[h.s2][:, :, :].rearrange("p a b -> p (a b)"), Traw[h.s2][:, ::-1],
                               ACT.Copy).then_inc(thi_done, 1)

            def x_hi(h, j):
                need(act, xt_done, h.n * 2 + j + 1)
                need(act, y_mm, (h.n - 1) * 2)
                act.activation(eo(Xhi[h.s2], j), psX[j][:, :], ACT.Copy).then_inc(xhi_done, 1)

            def x_even(h):
                need(act, xlo_even, h.n)
                act.activation(xeven[:, :], psX[0][:, :], ACT.Copy).then_inc(xeven_done, 1)

            def first_state(h):
                need(act, s_mm, h.n + 1)
                need(act, shi_done, h.n - 1)
                need(act, slo_done, h.n - 1)
                act.activation(Sf[h.s2][:, 0:P], psS[:, 0:P], ACT.Copy).then_inc(s0_copied, 1)

            def s_hi(h):
                need(act, s_carried, h.n * 2 + 2)
                need(act, y_mm, (h.n - 1) * 2)
                act.activation(Shi[h.s2][:, :], Sf[h.s2][:, :], ACT.Copy).then_inc(shi_done, 1)

            def w_hi(h):
                need(act, wh_turned, h.n + 1)
                need(act, up_mm, (h.n - 1) * 2)
                act.activation(whi[h.s2][:, :], psWh, ACT.Copy).then_inc(whi_done, 1)

            def step(head):
                if head(0).there and not is_head(head(0), 0):
                    first_state(head(0))
                if head(4).there:
                    turns(head(4))
                if head(3).there:
                    m_matrix(head(3))
                if head(1).there and not is_head(head(0), 0):
                    x_hi(head(1), 0)
                    x_hi(head(1), 1)
                if head(0).there and not is_head(head(0), 0):
                    s_hi(head(0))
                if head(1).there and not is_head(head(0), 0):
                    x_even(head(1))
                if head(2).there:
                    b_hi(head(2))
                if head(3).there:
                    sines(head(3))
                if head(1).there:
                    t_hi(head(1))
                if head(-1).there:
                    w_hi(head(-1))
                if head(3).there:
                    g_hi(head(3))

            first = [Head(0, n, 0) for n in range(4)]
            x_hi(first[0], 0)
            x_hi(first[0], 1)
            x_even(first[0])
            act.wait_ge(tabs_turned, 1)
            act.activation(tab1[:, :, :], psY[0][:, 0:4 * H].rearrange("p (t h) -> p t h", h=H),
                           ACT.Copy).then_inc(tab_done, 1)
            act.wait_ge(phases_done, 1)
            act.activation(sine[:, :, :], phase[:, :, :], ACT.Sin, scale=TURN).then_inc(sines_done, 1)
            act.activation(sine_half[:, :, :], phase[:, :, :], ACT.Sin, scale=TURN / 2).then_inc(sines_done, 1)
            act.wait_ge(consts, 10)
            act.wait_ge(tab_done, 1)
            turns(first[0])
            act.wait_ge(rho_done, 3)
            act.activation(magP[:, :, :], rho16[:, :, :], ACT.Exp, scale=float(G16)).then_inc(mag_done, 1)
            act.activation(magQ[:, :, :], rho16[:, :, :], ACT.Exp).then_inc(mag_done, 1)
            sines(first[0])
            act.wait_ge(tabs_turned, 2)
            act.activation(tab2[:, :, :], psY[1][:, 0:5 * H].rearrange("p (t h) -> p t h", h=H),
                           ACT.Copy).then_inc(tab_done, 1)
            act.wait_ge(tab_done, 2)
            m_matrix(first[0])
            turns(first[1])
            m_matrix(first[1])
            act.wait_ge(in_D, 16)
            b_hi(first[0])
            sines(first[1])
            turns(first[2])
            g_hi(first[0])
            b_hi(first[1])
            g_hi(first[1])
            for j in range(2):
                act.wait_ge(b_turned, j + 1)
                act.activation(Bw_hi[:, j * 512:(j + 1) * 512], psY[j][:, :],
                               ACT.Copy).then_inc(bhi_set, 1)
            t_hi(first[0])
            first_state(first[0])
            sines(first[2])
            m_matrix(first[2])
            x_hi(first[1], 0)
            x_hi(first[1], 1)
            x_even(first[1])
            turns(first[3])
            s_hi(first[0])
            g_hi(first[2])
            run_steps(act, step)

        @block.vector
        def _(dve):
            count = [0]

            def link(ins, but=0):
                count[0] += 1
                ins.then_inc(v_set, 1)
                dve.wait_ge(v_set, count[0] - but)

            TS, TT, STT = dve.tensor_scalar, dve.tensor_tensor, dve.scalar_tensor_tensor
            LOG2E, LN2_HI, LN2_LO = 1.4426950408889634, 0.693359375, -2.12194440e-4
            TAYLOR = (1 / 720, 1 / 120, 1 / 24, 1 / 6, 0.5, 1.0)

            def horner(p, r, c):
                return STT(p, p, c, r, ALU.add, ALU.mult)

            v, k, r, p, t = (ex[:, j, 0:N + 1] for j in range(5))
            dve.memset(quarter[0:N, :], -0.25).then_inc(cols_set, 1)
            dve.memset(quarter[N:P, :], 0.0).then_inc(cols_set, 1)
            dve.wait_ge(in_logs, 32)
            link(TS(v, logs[:, :], 88.0, -87.0, ALU.min, ALU.max))
            link(TS(k, v, LOG2E, ROUND, ALU.mult, ALU.add))
            link(TS(k, k, ROUND, None, ALU.subtract))
            link(STT(r, k, -LN2_HI, v, ALU.mult, ALU.add))
            link(STT(r, k, -LN2_LO, r, ALU.mult, ALU.add))
            link(TS(p, r, 1.0 / 5040, None, ALU.mult))
            link(horner(p, r, TAYLOR[0]))
            link(horner(p, r, TAYLOR[1]), 1)
            link(TS(t.bitcast(I32), k, 127.0, None, ALU.add), 1)
            link(horner(p, r, TAYLOR[2]), 1)
            link(TS(t.bitcast(I32), t.bitcast(I32), 23, None, ALU.logical_shift_left), 1)
            for c in TAYLOR[3:]:
                link(horner(p, r, c))
            STT(exps[:, :], p, 1.0, t, ALU.add, ALU.mult).then_inc(exps_set, 1)
            dve.wait_ge(exps_set, 1)
            dve.wait_ge(in_par, 32)
            ar, dt, Ai = exps[:, 0:N], exps[:, N:N + 1], A_im[:, :]
            link(TS(rr[:, 0:N], ar, dt, -1.0, ALU.mult, ALU.mult), 1)
            link(TS(w[:, :], Ai, dt, None, ALU.mult))

            v, k, r, p, t = (ex[:, j, :] for j in range(5))
            inv = 1.0 / (2.0 * np.pi)
            c1 = float(np.round(inv * 2**14) / 2**14)
            c2 = float(np.round((inv - c1) * 2**27) / 2**27)
            c3 = float(inv - c1 - c2)
            V0, VH0, VL0, rho = (pack1[:, j, 0, :] for j in (V, VH, VL, RHO))
            w1, v1 = w12[:, :].bitcast(F32), v12[:, :].bitcast(F32)
            scales = (1.0, float(Q))
            link(TS(rr[:, N:2 * N], rr[:, 0:N], float(Q), None, ALU.mult), 1)
            link(TS(V0, w[:, :], inv, None, ALU.mult), 1)
            link(TS(v, rr[:, :], 88.0, -87.0, ALU.min, ALU.max), 1)
            link(dve.tensor_copy(w12[:, :], w[:, :]), 1)
            link(TS(k, v, LOG2E, ROUND, ALU.mult, ALU.add), 1)
            link(TT(w2[:, :], w[:, :], w1, ALU.subtract), 1)
            link(TS(k, k, ROUND, None, ALU.subtract), 1)
            link(TS(err[:, :], w1, c1, None, ALU.mult), 1)
            link(STT(r, k, -LN2_HI, v, ALU.mult, ALU.add), 1)
            link(dve.tensor_copy(v12[:, :], V0), 1)
            link(STT(r, k, -LN2_LO, r, ALU.mult, ALU.add), 1)
            link(TT(err[:, :], v1, err[:, :], ALU.subtract), 1)
            link(TS(p, r, 1.0 / 5040, None, ALU.mult), 1)
            link(STT(err[:, :], w1, -c2, err[:, :], ALU.mult, ALU.add), 1)
            link(horner(p, r, TAYLOR[0]), 1)
            link(STT(err[:, :], w2[:, :], -c1, err[:, :], ALU.mult, ALU.add), 1)
            link(horner(p, r, TAYLOR[1]), 1)
            link(STT(err[:, :], w2[:, :], -c2, err[:, :], ALU.mult, ALU.add), 1)
            link(horner(p, r, TAYLOR[2]), 1)
            link(STT(VL0, w1, -c3, err[:, :], ALU.mult, ALU.add), 1)
            link(dve.tensor_copy(VH0, v1), 1)
            link(dve.tensor_copy(rho, rr[:, 0:N]), 1)
            link(horner(p, r, TAYLOR[3]))
            dve.tensor_copy(pack1[:, :, 1, :], pack1[:, :, 0, :]).then_inc(pack1_done, 1)
            for j, e in enumerate(scales):
                link(TS(turns_of[:, j, :], V0, e, ROUND, ALU.mult, ALU.add), 1)
            link(horner(p, r, TAYLOR[4]), 1)
            link(TS(turns_of[:, :, :], turns_of[:, :, :], ROUND, None, ALU.subtract), 1)
            link(horner(p, r, TAYLOR[5]), 1)
            for j, e in enumerate(scales):
                link(STT(phase[:, j, :], VH0, e, turns_of[:, j, :], ALU.mult, ALU.subtract), 1)
            link(TS(t.bitcast(I32), k, 127.0, None, ALU.add), 1)
            for j, e in enumerate(scales):
                link(STT(phase[:, j, :], VL0, -e, phase[:, j, :], ALU.mult, ALU.add), 1)
            link(TS(t.bitcast(I32), t.bitcast(I32), 23, None, ALU.logical_shift_left), 1)
            TS(phase[:, :, :], phase[:, :, :], 0.5, -0.5, ALU.min, ALU.max).then_inc(phases_done, 1)
            dve.wait_ge(v_set, count[0])
            link(STT(er[:, :], p, 1.0, t, ALU.add, ALU.mult), 1)
            e1, e256 = er[:, 0:N], er[:, N:2 * N]

            dve.wait_ge(den_set, 1)
            dve.reciprocal(rden[:, :], den[:, :]).then_inc(rden_set, 1)
            dve.wait_ge(rden_set, 1)
            TS(rden[:, :], rden[:, :], -2.0, None, ALU.mult).then_inc(rden_set, 1)
            dve.wait_ge(consts, 10)
            dve.wait_ge(tab_done, 1)
            exponents(dve, *RHO_PARTS[0])

            def over(t):
                return t.rearrange("h (a n) -> h a n", a=1).to_broadcast([H, 2, N])

            def whole_turns(h):
                need(dve, turns_done, h.n * 2 + 2)
                need(dve, frac1_done, h.n - 1)
                dve.tensor_scalar(whole[h.s2][:, :], turns_t[h.s2][:, :], ROUND, ROUND,
                                  ALU.add, ALU.subtract).then_inc(whole_done, 1)

            def fractions(h):
                need(dve, frac1_done, h.n + 1)
                need(dve, frac_done, h.n)
                dve.scalar_tensor_tensor(frac2[:, :], egrid[:, :], col(tab1[:, VL, :], h), frac1[h.s2][:, :],
                                         ALU.mult, ALU.add).then_inc(frac2_done, 1)

            def clamp(h):
                need(dve, frac2_done, h.n + 1)
                need(dve, wave_done, h.n - 1)
                dve.tensor_scalar(fraction[h.s2][:, :], frac2[:, :], -0.5, 0.5,
                                  ALU.max, ALU.min).then_inc(frac_done, 1)

            def x_lo(h):
                need(dve, xhi_done, h.n * 2 + 2)
                need(dve, y_mm, (h.n - 1) * 2)
                dve.tensor_tensor(eo(Xlo[h.s2], 1), psX[1][:, :], eo(Xhi[h.s2], 1).bitcast(F32),
                                  ALU.subtract).then_inc(xlo_odd, 1)

            def largest(h):
                need(dve, z_mm, h.n + 1)
                need(dve, gate_done, h.n)
                dve.reduce_max(top[:, :], psZ[:, 0:E], axis=AX.X).then_inc(top_done, 1)

            def first_largest(h):
                need(dve, top_done, h.n + 1)
                dve.scalar_tensor_tensor(rank[:, :], psZ[:, 0:E], top[:, :], desc[:, :],
                                         ALU.is_equal, ALU.mult).then_inc(rank_done, 1)

            def first_best(h):
                need(dve, rank_done, h.n + 1)
                dve.reduce_max(best[:, :], rank[:, :], axis=AX.X).then_inc(best_done, 1)

            def gates(h):
                need(dve, best_done, h.n + 1)
                need(dve, wh_done, h.n)
                dve.tensor_scalar(gate[:, :], rank[:, :], best[:, :], top[:, :],
                                  ALU.is_equal, ALU.mult).then_inc(gate_done, 1)

            def gated(h):
                need(dve, gate_done, h.n + 1)
                need(dve, wh_turned, h.n)
                dve.tensor_tensor(wh[:, :].rearrange("p (e r) -> p e r", r=R),
                                  psZ[:, E:NW].rearrange("p (e r) -> p e r", r=R),
                                  gate[:, :].rearrange("p (e a) -> p e a", a=1)
                                  .to_broadcast([P, E, R]), ALU.mult).then_inc(wh_done, 1)

            def carry(h):
                need(dve, s0_copied, h.n + 1)
                for j in range(NS - 1):
                    need(dve, s_carried, h.n * 2 + j)
                    old, new = slice(j * P, (j + 1) * P), slice((j + 1) * P, (j + 2) * P)
                    for to, fr in ((slice(0, N), slice(N, P)), (slice(N, P), slice(0, N))):
                        dve.scalar_tensor_tensor(brought[to, :], Sf[h.s2][fr, old],
                                                 tab2[fr, BR, bass.ds(h.n, 1)], psS[to, new],
                                                 ALU.mult, ALU.add).then_inc(brought_done, 1)
                    need(dve, brought_done, h.n * 4 + j * 2 + 2)
                    dve.scalar_tensor_tensor(Sf[h.s2][:, new], Sf[h.s2][:, old], col(tab2[:, LR, :], h),
                                             brought[:, :], ALU.mult, ALU.add).then_inc(s_carried, 1)

            def b_lo(h):
                need(dve, bhi_done, h.n + 1)
                need(dve, s_mm, h.n - 1)
                dve.tensor_tensor(Blo[h.s2][:, :, :], psB[:, :, 0:P], Bhi[h.s2][:, :, :].bitcast(F32),
                                  ALU.subtract).then_inc(blo_done, 1)

            def w_lo(h):
                need(dve, whi_done, h.n + 1)
                need(dve, up_mm, (h.n - 1) * 2)
                dve.tensor_tensor(wlo[h.s2][:, :], psWh, whi[h.s2][:, :].bitcast(F32),
                                  ALU.subtract).then_inc(wlo_done, 1)

            def cut(h, j):
                need(dve, y_mm, h.n * 2 + j + 1)
                need(dve, z_mm, h.n)
                dve.tensor_tensor(Y[:, j, :, :].rearrange("p a b -> p (a b)"), psY[j][:, :],
                                  mask[:, j, :, :].rearrange("p a b -> p (a b)"),
                                  ALU.mult).then_inc(y_masked, 1)

            def add(h, j):
                need(dve, up_mm, h.n * 2 + j + 1)
                need(dve, x_in[h.s4], h.quarter * 16 + 16)
                need(dve, o_out[h.s2], h.half * 16)
                half = slice(j * 512, (j + 1) * 512)
                dve.tensor_tensor(ost[h.s2][:, half], psO[j][:, :], xt[h.s4][:, half],
                                  ALU.add).then_inc(added, 1)

            def step(head):
                if head(0).there:
                    carry(head(0))
                if is_head(head(0), 0):
                    whole_turns(head(3))
                    x_lo(head(1))
                if head(-1).there:
                    largest(head(-1))
                if head(3).there:
                    fractions(head(3))
                if head(-1).there:
                    first_largest(head(-1))
                if head(3).there:
                    clamp(head(3))
                if head(-1).there:
                    first_best(head(-1))
                    gates(head(-1))
                    gated(head(-1))
                if head(1).there and not is_head(head(0), 0):
                    x_lo(head(1))
                if head(2).there:
                    b_lo(head(2))
                if head(-1).there:
                    w_lo(head(-1))
                if head(4).there:
                    whole_turns(head(4))
                if head(0).there:
                    cut(head(0), 0)
                    cut(head(0), 1)
                if head(-1).there:
                    add(head(-1), 0)
                    add(head(-1), 1)

            first = [Head(0, n, 0) for n in range(4)]
            dve.wait_ge(v_set, count[0])
            dve.wait_ge(sines_done, 2)
            link(TT(Lm1[:, 1, :], e1, sine[:, 0, :], ALU.mult), 1)
            link(STT(cm1[:, :, :], sine_half[:, :, :], -2.0, sine_half[:, :, :], ALU.mult, ALU.mult), 1)
            link(TT(pack2[:, BR, 0, :], sine[:, 1, :], e256, ALU.mult), 1)
            link(TT(em1[:, :], e1, cm1[:, 0, :], ALU.mult), 1)
            link(STT(pack2[:, LR, 0, :], cm1[:, 1, :], 1.0, e256, ALU.add, ALU.mult), 1)
            link(STT(Lm1[:, 0, :], e1, -1.0, em1[:, :], ALU.add, ALU.add), 1)
            whole_turns(first[0])
            dve.wait_ge(ca_set, 1)
            link(TT(prod[:, 1, :, :], CA[:, :, :], over(Lm1[:, 1, :]), ALU.mult), 1)
            link(TS(Lre[:, :], Lm1[:, 0, :], 1.0, None, ALU.add), 1)
            link(TT(prod[:, 0, :, :], CA[:, :, :], over(Lm1[:, 0, :]), ALU.mult))
            link(TT(pack2[:, CK, 0, :], prod[:, 0, 0, :], prod[:, 1, 1, :], ALU.subtract), 1)
            link(TT(pack2[:, CK, 1, :], prod[:, 0, 1, :], prod[:, 1, 0, :], ALU.add))
            link(dve.tensor_copy(pack2[:, LR, 1, :], pack2[:, LR, 0, :]), 1)
            link(TS(pack2[:, BR, 1, :], pack2[:, BR, 0, :], -1.0, None, ALU.mult), 1)
            fractions(first[0])
            link(TT(prod[:, 0, :, :], pack2[:, CK, :, :], over(Lre[:, :]), ALU.mult), 1)
            link(TT(prod[:, 1, :, :], pack2[:, CK, :, :], over(Lm1[:, 1, :]), ALU.mult))
            clamp(first[0])
            link(TT(pack2[:, M0, 0, :], prod[:, 0, 0, :], prod[:, 1, 1, :], ALU.subtract), 1)
            link(TT(pack2[:, M1, 0, :], prod[:, 0, 1, :], prod[:, 1, 0, :], ALU.add))
            dve.tensor_copy(pack2[:, M0, 1, :], pack2[:, M1, 0, :]).then_inc(pack2_done, 1)
            TS(pack2[:, M1, 1, :], pack2[:, M0, 0, :], -1.0, None, ALU.mult).then_inc(pack2_done, 1)
            whole_turns(first[1])
            x_lo(first[0])
            fractions(first[1])
            clamp(first[1])
            dve.wait_ge(w_turned, 1)
            dve.tensor_copy(Wt[:, 0:4, E:NW], psZ[:, :].rearrange("p (c w) -> p c w", w=P)).then_inc(w_done, 1)
            dve.tensor_copy(Wt[:, 4:8, E:NW], psO[1][:, :].rearrange("p (c w) -> p c w", w=P)).then_inc(w_done, 1)
            dve.tensor_copy(Wt[:, :, 0:E], psS[:, 0:NB * E].rearrange("p (c w) -> p c w", w=E)).then_inc(w_done, 1)
            b_lo(first[0])
            whole_turns(first[2])
            dve.wait_ge(in_len, 16)
            link(dve.tensor_copy(lens_f[:, :], lens_i[:, :]))
            for c in range(NB):
                TS(mask[:, c % 2, c // 2, :], lens_f[:, :], posn[:, c:c + 1], None,
                   ALU.is_gt).then_inc(mask_done, 1)
            b_lo(first[1])
            fractions(first[2])
            clamp(first[2])
            for j in range(2):
                dve.wait_ge(bhi_set, j + 1)
                TT(Bw_lo[:, j * 512:(j + 1) * 512], psY[j][:, :],
                   Bw_hi[:, j * 512:(j + 1) * 512].bitcast(F32), ALU.subtract).then_inc(blo_set, 1)
            dve.wait_ge(mask_done, NB)
            dve.wait_ge(tab_done, 2)
            run_steps(dve, step)

        @block.tensor
        def _(pe):
            def three(dst, pairs, first, last):
                n = 3 * len(pairs)
                i = 0
                for (ah, al), (bh, bl) in pairs:
                    for a, b in ((ah, bh), (ah, bl), (al, bh)):
                        mm = pe.matmul(dst, a, b, start=first and i == 0, stop=last and i == n - 1,
                                       skip_group_check=True)
                        i += 1
                return mm

            def turn_x(h, j):
                need(pe, x_in[h.s4], h.quarter * 16 + 16)
                need(pe, *((xlo_odd, h.n) if j else (xeven_done, h.n)))
                for c in range(NE):
                    at = (2 * c + j) * P
                    last = pe.transpose(psX[j][:, c * P:(c + 1) * P], xt[h.s4][:, at:at + P], ident[:, :])
                last.then_inc(xt_done, 1)

            def project(h, j):
                need(pe, y_masked, h.n * 2 + j + 1)
                if j == 0:
                    need(pe, wlo_done, h.n)
                for c in range(NE):
                    last = pe.matmul(psZ[:, 0:NW], Y[:, j, c, :], Wt[:, 2 * c + j, :],
                                     start=(j == 0 and c == 0), stop=(j == 1 and c == NE - 1),
                                     skip_group_check=True)
                if j == 1:
                    last.then_inc(z_mm, 1)

            def bring(h):
                need(pe, xhi_done, h.n * 2 + 2)
                need(pe, xlo_even, h.n + 1)
                need(pe, xlo_odd, h.n + 1)
                need(pe, bhi_done, h.n + 1)
                need(pe, blo_done, h.n + 1)
                need(pe, s_carried, h.n * 2)
                w = NS * P
                three(psS[:, 0:w],
                      [((Bhi[h.s2][:, j, :], Blo[h.s2][:, j, :]), (Xhi[h.s2][:, j, 0:w], Xlo[h.s2][:, j, 0:w]))
                       for j in range(2)], True, True).then_inc(s_mm, 1)

            def inputs(h):
                need(pe, added, (h.n - 3) * 2 - 1)
                need(pe, blo_done, h.n)
                need(pe, mx_done, h.n * 3 + 3)
                need(pe, grev_done, h.n + 1)
                for j in range(2):
                    last = pe.matmul(psB[:, j, :], Grev[h.s2][:, j * P:(j + 1) * P],
                                     Mx[h.s2][:, :], start=True, stop=True, skip_group_check=True)
                last.then_inc(b_mm, 1)

            def within(h, j):
                need(pe, thi_done, h.n + 1)
                need(pe, tlo_done, h.n + 1)
                T = [(Thi[h.s2][:, j, :], Tlo[h.s2][:, j, :]) for j in range(2)]
                X = [(Xhi[h.s2][:, j, :], Xlo[h.s2][:, j, :]) for j in range(2)]
                if is_head(h, 0):
                    pe.wait_ge(blo_set, j + 1)
                need(pe, y_masked, h.n * 2 - 1 + j)
                three(psY[j][:, :], [(T[0], X[j])] + [(T[1], X[0])] * j, True, False)

            def from_states(h):
                need(pe, shi_done, h.n + 1)
                need(pe, slo_done, h.n + 1)
                need(pe, glo_done, h.n + 1)
                for j in range(2):
                    G = tuple(g[h.s4][:, j * P:(j + 1) * P] for g in (Ghi, Glo))
                    three(psY[j][:, P:512], [(G, (Shi[h.s2][:, :], Slo[h.s2][:, :]))],
                          False, True).then_inc(y_mm, 1)

            def turn_wh(h):
                need(pe, wh_done, h.n + 1)
                need(pe, wlo_done, h.n)
                pe.transpose(psWh, wh[:, :], ident[:, :]).then_inc(wh_turned, 1)

            def up(h, ahead):
                need(pe, whi_done, h.n + 1)
                need(pe, wlo_done, h.n + 1)
                if ahead.there:
                    need(pe, blo_done, ahead.n + 1)
                for j in range(2):
                    need(pe, added, h.n * 2 - 1 + j)
                    half = slice(j * 512, (j + 1) * 512)
                    three(psO[j][:, :], [((whi[h.s2][:, :], wlo[h.s2][:, :]),
                                          (Bw_hi[:, half], Bw_lo[:, half]))],
                          True, True).then_inc(up_mm, 1)

            def step(head):
                if head(0).there:
                    bring(head(0))
                if head(-1).there:
                    project(head(-1), 0)
                    project(head(-1), 1)
                if head(1).there:
                    turn_x(head(1), 0)
                    turn_x(head(1), 1)
                if head(2).there and not is_head(head(0), 0):
                    inputs(head(2))
                if head(0).there:
                    within(head(0), 0)
                    within(head(0), 1)
                if is_head(head(0), 0):
                    inputs(head(2))
                if head(-1).there:
                    turn_wh(head(-1))
                if head(0).there:
                    from_states(head(0))
                if head(-1).there:
                    up(head(-1), head(2))

            def turn_tables(pack, bank_, n):
                for t in range(n):
                    last = pe.transpose(bank_[:, t * H:(t + 1) * H],
                                        pack[:, t, :, :].rearrange("h a n -> h (a n)"), ident[0:H, 0:H])
                last.then_inc(tabs_turned, 1)

            first = [Head(0, n, 0) for n in range(2)]
            pe.wait_ge(consts, 10)
            turn_x(first[0], 0)
            turn_x(first[0], 1)
            pe.wait_ge(pack1_done, 1)
            turn_tables(pack1, psY[0], 4)
            pe.wait_ge(in_A, 16)
            pe.wait_ge(in_rw, 16)
            for c in range(NB):
                cols = slice((c % 4) * P, (c % 4 + 1) * P)
                pe.transpose((psO[1] if c // 4 else psZ)[:, cols], A_nat[:, c * P:(c + 1) * P], ident[:, :])
            for c in range(NB):
                last = pe.transpose(psS[:, c * E:(c + 1) * E], route_nat[:, c * P:(c + 1) * P],
                                    ident[0:E, 0:E])
            last.then_inc(w_turned, 1)
            pe.wait_ge(pack2_done, 2)
            turn_tables(pack2, psY[1], 5)
            inputs(first[0])
            pe.wait_ge(in_B, 16 * E)
            for c in range(NB):
                cols = slice((c % 4) * P, (c % 4 + 1) * P)
                if c % 4 == 0:
                    pe.wait_ge(tab_done, c // 4 + 1)
                last = pe.transpose(psY[c // 4][:, cols], B_nat[:, c, :], ident[:, :])
                if c % 4 == 3:
                    last.then_inc(b_turned, 1)
            inputs(first[1])
            pe.wait_ge(w_done, 3)
            run_steps(pe, step)


_INS = ['x', 'itok_B_8_3872', 'L0_cond_log_dt', 'L0_cond_C', 'L0_cond_log_A_real', 'L0_cond_A_imag',
        'L0_cond_D', 'L0_ffn_route_w', 'L0_ffn_A', 'L0_ffn_Bw']


def kernel(**inputs):
    import numpy as _np
    import concourse.bacc as _bacc
    from concourse import mybir as _mybir
    from concourse.bass_utils import run_bass_kernel_spmd as _run

    nc = _bacc.Bacc("TRN2", target_bir_lowering=False, num_devices=1)
    arrays, args = {}, []
    for name in _INS:
        a = _np.ascontiguousarray(inputs[name])
        arrays[f"in_{name}_dram"] = a
        args.append(nc.dram_tensor(f"in_{name}_dram", a.shape, _mybir.dt.from_np(a.dtype), kind="ExternalInput").ap())
    shape = inputs['x'].shape
    args.append(nc.dram_tensor("out_0_dram", shape, _mybir.dt.float32, kind="ExternalOutput").ap())
    conv_ffn_kernel(nc, *args)
    r = _run(nc, [arrays], core_ids=[0])
    return r.results[0]["out_0_dram"]
```
